# Optimizing a Trainium2 kernel written in Bass

```python
import numpy as np
import jax
import jax.numpy as jnp

def _softmax(x, axis=-1):
    return jax.nn.softmax(x, axis=axis)

def _gelu(x):
    return jax.nn.gelu(x, approximate=True)

def _silu(x):
    return jax.nn.silu(x)

def _sigmoid(x):
    return jax.nn.sigmoid(x)

def _layernorm(x, axis=-1, eps=1e-05):
    m = jnp.mean(x, axis=axis, keepdims=True)
    v = jnp.var(x, axis=axis, keepdims=True)
    return (x - m) / jnp.sqrt(v + eps)

def _scatter_add(tgt, idx, src, axis=0):
    return tgt.at[idx].add(src)

def _segment_sum(src, seg, n):
    return jax.ops.segment_sum(src, seg, n)
kernel_name = 'mk_adj_resnorm_d1_adj_r2_06c082'

def setup_inputs(seed: int=0):
    np.random.seed(seed)
    _w = jnp.asarray

    def _rec_inputs():
        import jax
        import jax.numpy as jnp
        _gk = jax.random.key(seed)
        x = -0.0002928 + 1 * jax.random.normal(jax.random.fold_in(_gk, 1), (8, 2048, 128), jnp.float32)
        _a = jax.random.bernoulli(jax.random.fold_in(_gk, 2), 0.0078125, (8, 2048, 2048))
        _a = jnp.logical_or(_a, jnp.eye(2048, dtype=bool))
        _af = _a.astype(jnp.float32)
        _af = _af * jax.random.uniform(jax.random.fold_in(_gk, 3), (8, 2048, 2048), jnp.float32, 0.05, 1)
        adj = _af
        return (x, adj)
    x, adj = _rec_inputs()

    def _L0_gnn_setup():
        import jax, jax.numpy as jnp
        import numpy as np
        ALPHA = 0.2
        MLP_ALPHA = 0.01
        EPS = 1e-05

        def leaky(x, a):
            return jnp.where(x >= 0, x, a * x)
        key = jax.random.key(seed)
        ks = jax.random.split(key, 12)
        B, N, FIN, FOUT, K = (4, 2048, 128, 128, 64)
        s = 0.05
        return {'h': jax.random.normal(ks[0], (B, N, FIN), jnp.float32), 'adj': jax.random.uniform(ks[1], (B, N, N), jnp.float32), 'W': jax.random.normal(ks[2], (FIN, FOUT), jnp.float32) * s, 'a': jax.random.normal(ks[3], (FOUT, 1), jnp.float32) * s, 'ln_g': jnp.ones((FOUT,), jnp.float32), 'ln_b': jnp.zeros((FOUT,), jnp.float32), 'W1': jax.random.normal(ks[4], (FOUT, FOUT), jnp.float32) * s, 'b1': jnp.zeros((FOUT,), jnp.float32), 'W2': jax.random.normal(ks[5], (FOUT, FOUT), jnp.float32) * s, 'b2': jnp.zeros((FOUT,), jnp.float32), 'W3': jax.random.normal(ks[6], (FOUT, FOUT), jnp.float32) * s, 'b3': jnp.zeros((FOUT,), jnp.float32), 'k': K}
    _L0_gnn_all = _L0_gnn_setup()
    _L0_gnn_in = {k: v for k, v in _L0_gnn_all.items() if k in ('W', 'a', 'ln_g', 'ln_b', 'W1', 'b1', 'W2', 'b2', 'W3', 'b3')}
    del _L0_gnn_all
    return {'x': x, 'adj': adj, 'L0_gnn_W': _L0_gnn_in['W'], 'L0_gnn_a': _L0_gnn_in['a'], 'L0_gnn_ln_g': _L0_gnn_in['ln_g'], 'L0_gnn_ln_b': _L0_gnn_in['ln_b'], 'L0_gnn_W1': _L0_gnn_in['W1'], 'L0_gnn_b1': _L0_gnn_in['b1'], 'L0_gnn_W2': _L0_gnn_in['W2'], 'L0_gnn_b2': _L0_gnn_in['b2'], 'L0_gnn_W3': _L0_gnn_in['W3'], 'L0_gnn_b3': _L0_gnn_in['b3']}

def reference(x, adj, L0_gnn_W, L0_gnn_a, L0_gnn_ln_g, L0_gnn_ln_b, L0_gnn_W1, L0_gnn_b1, L0_gnn_W2, L0_gnn_b2, L0_gnn_W3, L0_gnn_b3):
    import jax
    import jax.numpy as jnp

    def _L0_gnn_ref(h, adj, W, a, ln_g, ln_b, W1, b1, W2, b2, W3, b3, k):
        import jax, jax.numpy as jnp
        import numpy as np
        ALPHA = 0.2
        MLP_ALPHA = 0.01
        EPS = 1e-05

        def leaky(x, a):
            return jnp.where(x >= 0, x, a * x)
        Wh = h @ W
        B, N, Fd = Wh.shape
        C = N // k
        Whc = Wh.reshape(B, C, k, Fd)
        e = leaky(jnp.squeeze(Whc @ a, -1), ALPHA)
        idx = jnp.arange(C)
        blocks = adj.reshape(B, C, k, C, k)[:, idx, :, idx, :]
        blocks = jnp.transpose(blocks, (1, 0, 2, 3))
        scores = jax.nn.softmax(blocks * e[..., :, None], axis=-1)
        out = jnp.einsum('bcij,bcjf->bcif', scores, Whc)
        y = leaky(out @ W1 + b1, MLP_ALPHA)
        y = leaky(y @ W2 + b2, MLP_ALPHA)
        y = y @ W3 + b3
        z = y + out
        mu = jnp.mean(z, axis=-1, keepdims=True)
        var = jnp.var(z, axis=-1, keepdims=True)
        z = (z - mu) / jnp.sqrt(var + EPS) * ln_g + ln_b
        return z.reshape(B, N, Fd)
    x = _layernorm(x + _L0_gnn_ref(x, adj, L0_gnn_W, L0_gnn_a, L0_gnn_ln_g, L0_gnn_ln_b, L0_gnn_W1, L0_gnn_b1, L0_gnn_W2, L0_gnn_b2, L0_gnn_W3, L0_gnn_b3, 64), axis=-1)
    return x

_drawn_inputs = setup_inputs


def setup_inputs(seed=0):
    import zlib

    import numpy as np

    out = dict(_drawn_inputs(seed))
    spreads = {'L0_gnn_ln_g': (1.0, 0.2),
     'L0_gnn_ln_b': (0.0, 0.1),
     'L0_gnn_b1': (0.0, 0.1),
     'L0_gnn_b2': (0.0, 0.1),
     'L0_gnn_b3': (0.0, 0.1)}
    factors = {'adj': 6.205, 'L0_gnn_a': 5.857}
    for name, (base, spread) in spreads.items():
        noise = np.random.default_rng([zlib.crc32(name.encode()), seed]).standard_normal(out[name].shape)
        drawn = base * np.exp(spread * noise) if base else spread * noise
        out[name] = jnp.asarray(drawn.astype(out[name].dtype))
    for name, factor in factors.items():
        out[name] = (out[name] * factor).astype(out[name].dtype)
    return out
```

```python
import concourse.bass as bass
from concourse import mybir
from contextlib import ExitStack

B, N, F, BLK = 8, 2048, 128, 64
P = 128
TG = 4
ROWS = TG * P
GROUPS = B * N // ROWS
GPB = N // ROWS
BG = ROWS // BLK
EPS = 1e-5
SLOPE_E, SLOPE = 0.2, 0.01
FIRST, LAST = -2, GROUPS + 3
LOOP_FROM, LOOP_TO = 6, 30


class Group:

    def __init__(self, i, k):
        self.i, self.k = i, k

    def __add__(self, d):
        return Group(self.i, self.k + d)

    def __sub__(self, d):
        return Group(self.i, self.k - d)

    def real(self):
        return not isinstance(self.i, int) or 0 <= 4 * self.i + self.k < GROUPS

    def ring(self, size):
        return self.k % size

    def batch(self):
        return self.i + self.k // GPB

    def done(self, per=1):
        return self.i * (4 * per) + (self.k + 1) * per

    def dma_done(self, dmas=1):
        return (self.i + self.k // 4 + 1) * (16 * dmas)


def wait(eng, sem, group, per=1):
    if isinstance(group.i, int) and group.done(per) <= 0:
        return
    eng.wait_ge(sem, group.done(per))


def slots(eng, slot, late=0):
    for n in range(FIRST, LOOP_FROM - late):
        slot(Group(0, n))
    with eng.Fori(LOOP_FROM // 4, LOOP_TO // 4) as i:
        for k in range(4):
            slot(Group(i, LOOP_FROM % 4 + k - late))
    for n in range(LOOP_TO - late, LAST + 1):
        slot(Group(0, n))


def program(nc, x, adj, W, a, ln_g, ln_b, W1, b1, W2, b2, W3, b3, out):
    f32, bf16 = mybir.dt.float32, mybir.dt.bfloat16
    ALU, ACT, AX = mybir.AluOpType, mybir.ActivationFunctionType, mybir.AxisListType

    ctx = ExitStack()
    with ctx:
        def sb(name, shape, dt=f32):
            return ctx.enter_context(nc.sbuf_tensor(name, shape, dt))

        def ps(name, shape, dt=f32):
            return ctx.enter_context(nc.psum_tensor(name, shape, dt))

        def sem(name):
            return ctx.enter_context(nc.semaphore(name))

        W_sb, W1_sb, W2_sb, W3_sb = (sb(f"{n}_sb", [P, F]) for n in ("W", "W1", "W2", "W3"))
        a_sb, b1_sb, b2_sb = (sb(f"{n}_sb", [P, 1]) for n in ("a", "b1", "b2"))
        g_bc, b_bc, b3_bc = (sb(f"{n}_bc", [P, F]) for n in ("g", "b", "b3"))
        WT = sb("WT", [P, F])
        WW1 = sb("WW1", [P, F])
        wa_bc = sb("wa_bc", [P, F])
        a_wide = sb("a_wide", [P, P])
        Wc, W3c, b3c = sb("Wc", [P, F]), sb("W3c", [P, F]), sb("b3c", [P, F])
        wmean = sb("wmean", [P, 3])
        ident = sb("ident", [P, P])
        ones_f = sb("ones_f", [P, P])
        ones = sb("ones", [P, P], bf16)
        b3_hi, b3_mid, b3_lo = (sb(f"b3_{n}", [P, F], bf16) for n in ("hi", "mid", "lo"))
        b3_rest, b3_rest2 = sb("b3_rest", [P, F]), sb("b3_rest2", [P, F])
        b3_rows = sb("b3_rows", [P, TG, F], bf16)
        b3_sel = sb("b3_sel", [P, F])
        b3_sel2 = sb("b3_sel2", [P, F])
        eps = sb("eps", [P, 1])

        xt = [sb(f"x{i}", [P, TG, F]) for i in range(4)]
        at = [sb(f"adj{i}", [P, TG, BLK]) for i in range(4)]
        xw = [sb(f"xw{i}", [P, TG, F]) for i in range(2)]
        e_x = [sb(f"e_x{i}", [P, TG]) for i in range(2)]
        e_adj = [sb(f"e_adj{i}", [P, TG]) for i in range(2)]
        score = [sb(f"score{i}", [P, TG, BLK]) for i in range(2)]
        smax = [sb(f"smax{i}", [P, TG]) for i in range(2)]
        prob = [sb(f"prob{i}", [P, TG, BLK]) for i in range(2)]
        psum_ = [sb(f"probsum{i}", [P, TG]) for i in range(2)]
        pinv = [sb(f"probinv{i}", [P, TG]) for i in range(2)]
        pT = [sb(f"pT{i}", [P, TG, 2, BLK]) for i in range(2)]
        sx = [sb(f"sx{i}", [P, ROWS]) for i in range(2)]
        y1 = [sb(f"y1_{i}", [P, ROWS]) for i in range(2)]
        y2 = [sb(f"y2_{i}", [P, ROWS]) for i in range(2)]
        low1 = [sb(f"low1_{i}", [P, ROWS]) for i in range(2)]
        low2 = [sb(f"low2_{i}", [P, ROWS]) for i in range(2)]
        b1_low, b2_low = sb("b1_low", [P, 1]), sb("b2_low", [P, 1])
        junk = sb("junk", [P, 2, TG, F])
        ssq = [sb(f"ssq{i}", [P, TG]) for i in range(2)]
        u = [sb(f"u{i}", [P, TG, F]) for i in range(4)]
        t1 = [sb(f"t{i}", [P, TG, F]) for i in range(2)]
        r = [sb(f"r{i}", [P, TG, F]) for i in range(2)]
        stats = sb("stats", [P, 2, TG, 6])
        mv = [sb(f"mv{i}", [P, TG, 2]) for i in range(2)]
        o = [sb(f"o{i}", [P, TG, F]) for i in range(4)]
        small = lambda n: [[sb(f"{n}{j}{i}", [P, TG]) for i in range(2)] for j in range(2)]
        var, lnv, y0, y0sq, corr, rstd = (small(n) for n in ("var", "lnv", "y0_", "y0sq", "corr", "rstd"))
        nmr = [sb(f"nmr{i}", [P, TG]) for i in range(2)]

        pt_ps = [ps(f"pt_ps{i}", [P, 512]) for i in range(2)]
        sx_ps, y1_ps, y2_ps = ps("sx_ps", [P, 512]), ps("y1_ps", [P, 512]), ps("y2_ps", [P, 512])
        z_ps = [ps(f"z_ps{i}", [P, TG, F]) for i in range(2)]

        w_loaded = sem("w_loaded")
        const_made = sem("const_made")
        setup_pe = sem("setup_pe")
        setup_dve = sem("setup_dve")
        x_loaded = [sem(f"x_loaded{i}") for i in range(4)]
        adj_loaded = [sem(f"adj_loaded{i}") for i in range(4)]
        stored = [sem(f"stored{i}") for i in range(4)]
        xw_made = sem("xw_made")
        e_summed = sem("e_summed")
        e_made = sem("e_made")
        scaled = sem("scaled")
        max_made = sem("max_made")
        shifted = sem("shifted")
        exp_made = sem("exp_made")
        sum_made = sem("sum_made")
        inv_made = sem("inv_made")
        prob_made = sem("prob_made")
        transposed = sem("transposed")
        pT_made = sem("pT_made")
        sx_done = sem("sx_done")
        sx_made = sem("sx_made")
        l1_done = sem("l1_done")
        low1_made = sem("low1_made")
        low2_made = sem("low2_made")
        y1_made = sem("y1_made")
        l2_done = sem("l2_done")
        y2_made = sem("y2_made")
        z_done = sem("z_done")
        ssq_made = sem("ssq_made")
        u_made = sem("u_made")
        t_made = sem("t_made")
        r_made = sem("r_made")
        stats_made = sem("stats_made")
        mv_made = sem("mv_made")
        var_made, ln_made, y0_made, sq_made, corr_made, rstd_made = (
            [sem(f"{n}{j}") for j in range(2)]
            for n in ("var_made", "ln_made", "y0_made", "sq_made", "corr_made", "rstd_made"))
        nmr_made = sem("nmr_made")
        o_made = sem("o_made")

        x_flat = x.rearrange("b n f -> (b n) f")
        out_flat = out.rearrange("b n f -> (b n) f")

        def rows_of(flat, g):
            return bass.AP(tensor=flat.tensor, offset=g.i * (4 * ROWS * F) + g.k * (ROWS * F),
                           ap=[[F, P], [P * F, TG], [1, F]])

        def blocks_of(g, b):
            step = BLK * (N + 1)
            return bass.AP(tensor=adj.tensor, offset=g.batch() * (N * N) + ((g.k % GPB) * BG + 4 * b) * step,
                           ap=[[N, BLK], [step, 4], [1, BLK]])

        def wide(v):
            return v[:, :].rearrange("p (s o) -> p s o", o=1).broadcast_to([P, TG, BLK])

        def each_tile(v):
            return v[:, :].rearrange("p (o f) -> p o f", o=1).broadcast_to([P, TG, F])

        block = ctx.enter_context(nc.Block())

        @block.sync
        def _(sync):
            def load(g):
                if not g.real():
                    return
                wait(sync, sx_done, g - 4)
                wait(sync, u_made, g - 4)
                sync.dma_start(xt[g.ring(4)][:, :, :], rows_of(x_flat, g)).then_inc(x_loaded[g.ring(4)], 16)
                wait(sync, scaled, g - 4)
                for b in range(2):
                    sync.dma_start(at[g.ring(4)][BLK * b:BLK * b + BLK, :, :],
                                   blocks_of(g, b)).then_inc(adj_loaded[g.ring(4)], 16)

            def slot(n):
                load(n + 4)
                g = n - 4
                if g.real():
                    wait(sync, o_made, g)
                    sync.dma_start(rows_of(out_flat, g), o[g.ring(4)][:, :, :]).then_inc(stored[g.ring(4)], 16)

            load(Group(0, 0))
            weights = [(W_sb, W), (a_sb, a), (W1_sb, W1), (W3_sb, W3), (W2_sb, W2)]
            for dst, src in weights:
                sync.dma_start(dst[:, :], src[:, :]).then_inc(w_loaded, 16)
            for dst, src in ((b1_sb, b1), (b2_sb, b2)):
                sync.dma_start(dst[:, :], src.rearrange("(p o) -> p o", o=1)).then_inc(w_loaded, 16)
            for dst, src in ((g_bc, ln_g), (b_bc, ln_b), (b3_bc, b3)):
                sync.dma_start(dst[:, :], src.rearrange("(o f) -> o f", o=1).broadcast_to([P, F])).then_inc(w_loaded, 16)
            load(Group(0, 1))
            slots(sync, slot, late=2)
            for k in range(4):
                sync.wait_ge(stored[k], 16 * (GROUPS // 4))

        @block.gpsimd
        def _(pool):
            pool.memset(ident[:, :], 0.0).then_inc(const_made, 1)
            pool.memset(ones_f[:, :], 1.0).then_inc(const_made, 1)
            pool.wait_ge(const_made, 1)
            pool.affine_select(out=ident[:, :], in_=ident[:, :], compare_op=ALU.not_equal, fill=1.0,
                               base=0, pattern=[[-1, P]], channel_multiplier=1).then_inc(const_made, 1)
            pool.memset(ones[:, :], 1.0).then_inc(const_made, 1)
            pool.memset(eps[:, :], EPS).then_inc(const_made, 1)
            pool.memset(b3_rows[:, :, :], 0.0).then_inc(const_made, 1)
            for i in range(2):
                pool.memset(pT[i][:, :, :, :], 0.0).then_inc(const_made, 1)
            pool.wait_ge(setup_dve, 3)

            def slot(n):
                g = n - 4
                if g.real():
                    wait(pool, r_made, g)
                    if not isinstance(g.i, int) or g.k >= 4:
                        pool.wait_ge(stored[g.ring(4)], (g - 4).dma_done())
                g = n + 1
                if g.real():
                    wait(pool, inv_made, g)
                    wait(pool, exp_made, g)
                    pool.tensor_tensor(prob[g.ring(2)][:, :, :], prob[g.ring(2)][:, :, :],
                                       wide(pinv[g.ring(2)]), ALU.mult).then_inc(prob_made, 1)
                g = n + 2
                if g.real():
                    pool.wait_ge(x_loaded[g.ring(4)], g.dma_done())
                    wait(pool, e_summed, g - 2)
                    pool.tensor_tensor(xw[g.ring(2)][:, :, :], xt[g.ring(4)][:, :, :], each_tile(wa_bc),
                                       ALU.mult).then_inc(xw_made, 1)
                g = n - 4
                if g.real():
                    pool.wait_ge(const_made, 8)
                    wait(pool, rstd_made[1], g)
                    wait(pool, nmr_made, g)
                    for s in range(TG):
                        last = pool.tensor_scalar(o[g.ring(4)][:, s, :], r[g.ring(2)][:, s, :],
                                                  rstd[1][g.ring(2)][:, s:s + 1], nmr[g.ring(2)][:, s:s + 1],
                                                  op0=ALU.mult, op1=ALU.add)
                    last.then_inc(o_made, 1)
                g = n + 2
                if g.real():
                    pool.wait_ge(adj_loaded[g.ring(4)], g.dma_done(2))
                    wait(pool, e_made, g, 4)
                    wait(pool, exp_made, g - 2)
                    pool.tensor_tensor(score[g.ring(2)][:, :, :], at[g.ring(4)][:, :, :],
                                       wide(e_adj[g.ring(2)]), ALU.mult).then_inc(scaled, 1)
                    wait(pool, max_made, g)
                    wait(pool, scaled, g)
                    pool.tensor_tensor(score[g.ring(2)][:, :, :], score[g.ring(2)][:, :, :],
                                       wide(smax[g.ring(2)]), ALU.subtract).then_inc(shifted, 1)

            slots(pool, slot)

        @block.vector
        def _(dve):
            dve.wait_ge(w_loaded, 16 * 10)
            dve.wait_ge(const_made, 8)
            V = nc.vector
            V.tensor_scalar(a_wide[:, :], ones_f[:, :], a_sb[:, 0:1], None, op0=ALU.mult).then_inc(setup_dve, 1)
            dve.wait_ge(setup_pe, 1)
            V.tensor_copy(WT[:, :], sx_ps[:, 0:P]).then_inc(setup_dve, 1)
            dve.wait_ge(setup_pe, 2)
            V.tensor_copy(wa_bc[:, :], y1_ps[:, 0:F]).then_inc(setup_dve, 1)
            dve.wait_ge(setup_pe, 3)
            V.tensor_copy(WW1[:, :], y2_ps[:, 0:F]).then_inc(setup_dve, 1)
            done = 4
            for j, (src, dst) in enumerate(((W_sb, Wc), (W3_sb, W3c), (b3_bc, b3c))):
                V.tensor_reduce(wmean[:, j:j + 1], src[:, :], op=ALU.add, axis=AX.X).then_inc(setup_dve, 1)
                dve.wait_ge(setup_dve, done + 1)
                V.tensor_scalar(wmean[:, j:j + 1], wmean[:, j:j + 1], 1.0 / F, None, op0=ALU.mult).then_inc(setup_dve, 1)
                dve.wait_ge(setup_dve, done + 2)
                V.tensor_scalar(dst[:, :], src[:, :], wmean[:, j:j + 1], None, op0=ALU.subtract).then_inc(setup_dve, 1)
                done += 3

            def then(instruction):
                nonlocal done
                instruction.then_inc(setup_dve, 1)
                done += 1
                dve.wait_ge(setup_dve, done)

            dve.wait_ge(setup_dve, done)
            then(V.tensor_copy(b3_hi[:, :], b3c[:, :]))
            then(V.tensor_tensor(b3_rest[:, :], b3c[:, :], b3_hi[:, :], ALU.subtract))
            then(V.tensor_copy(b3_mid[:, :], b3_rest[:, :]))
            then(V.tensor_tensor(b3_rest2[:, :], b3_rest[:, :], b3_mid[:, :], ALU.subtract))
            then(V.tensor_copy(b3_lo[:, :], b3_rest2[:, :]))
            then(V.tensor_scalar(b3_sel[:, :], b3_hi[:, :], ident[:, 0:1], None, op0=ALU.mult))
            then(V.scalar_tensor_tensor(b3_sel2[:, :], b3_mid[:, :], ident[:, 1:2], b3_sel[:, :], op0=ALU.mult, op1=ALU.add))
            then(V.scalar_tensor_tensor(b3_sel[:, :], b3_lo[:, :], ident[:, 2:3], b3_sel2[:, :], op0=ALU.mult, op1=ALU.add))
            V.tensor_copy(b3_rows[:, :, :], each_tile(b3_sel)).then_inc(setup_dve, 1)
            V.tensor_scalar(b1_low[:, :], b1_sb[:, :], SLOPE, None, op0=ALU.mult).then_inc(setup_dve, 1)
            V.tensor_scalar(b2_low[:, :], b2_sb[:, :], SLOPE, None, op0=ALU.mult).then_inc(setup_dve, 1)

            def newton(j, g, step):
                q = g.ring(2)
                if step == 0:
                    wait(dve, y0_made[j], g)
                    V.tensor_tensor(y0sq[j][q][:, :], y0[j][q][:, :], y0[j][q][:, :], ALU.mult).then_inc(sq_made[j], 1)
                elif step == 1:
                    wait(dve, sq_made[j], g)
                    V.scalar_tensor_tensor(corr[j][q][:, :], y0sq[j][q][:, :], -0.5, var[j][q][:, :],
                                           op0=ALU.mult, op1=ALU.mult).then_inc(corr_made[j], 1)
                else:
                    wait(dve, corr_made[j], g)
                    V.scalar_tensor_tensor(rstd[j][q][:, :], corr[j][q][:, :], 1.5, y0[j][q][:, :],
                                           op0=ALU.add, op1=ALU.mult).then_inc(rstd_made[j], 1)

            def leaky(dst, src_ps, bias, low):
                return V.scalar_tensor_tensor(dst[:, :], src_ps[:, :], bias[:, 0:1], low[:, :], op0=ALU.add, op1=ALU.max)

            def slot(n):
                up, cur, prev, n1, n2 = n + 1, n, n - 1, n - 3, n - 4
                front = n + 2
                if up.real():
                    q = up.ring(2)
                    wait(dve, exp_made, up)
                    V.tensor_reduce(psum_[q][:, :], prob[q][:, :, :], op=ALU.add, axis=AX.X).then_inc(sum_made, 1)
                if n1.real():
                    q = n1.ring(2)
                    wait(dve, ssq_made, n1, TG)
                    V.tensor_scalar(var[0][q][:, :], ssq[q][:, :], 1.0 / F, EPS, op0=ALU.mult,
                                    op1=ALU.add).then_inc(var_made[0], 1)
                    newton(0, n1, 0)
                if up.real():
                    q = up.ring(2)
                    wait(dve, sum_made, up)
                    V.reciprocal(pinv[q][:, :], psum_[q][:, :]).then_inc(inv_made, 1)
                if n1.real():
                    wait(dve, var_made[0], n1)
                    newton(0, n1, 1)
                if n2.real():
                    newton(1, n2, 0)
                if n1.real():
                    newton(0, n1, 2)
                if n2.real():
                    newton(1, n2, 1)
                if cur.real():
                    dve.wait_ge(x_loaded[cur.ring(4)], cur.dma_done())
                    wait(dve, r_made, cur - 4)
                    V.tensor_tensor(u[cur.ring(4)][:, :, :], xt[cur.ring(4)][:, :, :], each_tile(b_bc),
                                    ALU.add).then_inc(u_made, 1)
                if n2.real():
                    newton(1, n2, 2)
                if n1.real():
                    q = n1.ring(2)
                    wait(dve, rstd_made[0], n1)
                    wait(dve, r_made, n1 - 2)
                    for s in range(TG):
                        last = V.scalar_tensor_tensor(t1[q][:, s, :], z_ps[q][:, s, :], rstd[0][q][:, s:s + 1],
                                                      g_bc[:, :], op0=ALU.mult, op1=ALU.mult)
                    last.then_inc(t_made, 1)
                if prev.real():
                    q = prev.ring(2)
                    wait(dve, low2_made, prev)
                    wait(dve, z_done, prev - 2)
                    leaky(y2[q], y2_ps, b2_sb, low2[q]).then_inc(y2_made, 1)
                if n2.real():
                    q = n2.ring(2)
                    wait(dve, rstd_made[1], n2)
                    V.scalar_tensor_tensor(nmr[q][:, :], mv[q][:, :, 0], -1.0, rstd[1][q][:, :],
                                           op0=ALU.mult, op1=ALU.mult).then_inc(nmr_made, 1)
                if front.real():
                    q = front.ring(2)
                    wait(dve, xw_made, front)
                    wait(dve, e_made, front - 2, 4)
                    V.tensor_reduce(e_x[q][:, :], xw[q][:, :, :], op=ALU.add, axis=AX.X).then_inc(e_summed, 1)
                if n1.real():
                    q = n1.ring(2)
                    wait(dve, t_made, n1)
                    wait(dve, u_made, n1)
                    wait(dve, o_made, n1 - 2)
                    V.tensor_tensor(r[q][:, :, :], t1[q][:, :, :], u[n1.ring(4)][:, :, :], ALU.add).then_inc(r_made, 1)
                if front.real():
                    q = front.ring(2)
                    wait(dve, e_summed, front)
                    wait(dve, scaled, front - 2)
                    for b in range(2):
                        for t in range(2):
                            src = e_x[q][BLK * t:BLK * t + BLK, 2 * b:2 * b + 2]
                            V.scalar_tensor_tensor(e_adj[q][BLK * b:BLK * b + BLK, t:TG:2], src, SLOPE_E, src,
                                                   op0=ALU.mult, op1=ALU.max).then_inc(e_made, 1)
                if n1.real():
                    q = n1.ring(2)
                    wait(dve, r_made, n1)
                    wait(dve, mv_made, n1 - 2)
                    for s in range(TG):
                        last = V.bn_stats(stats[:, q, s, :], r[q][:, s, :])
                    last.then_inc(stats_made, 1)
                if front.real():
                    q = front.ring(2)
                    wait(dve, scaled, front)
                    wait(dve, shifted, front - 2)
                    V.tensor_reduce(smax[q][:, :], score[q][:, :, :], op=ALU.max, axis=AX.X).then_inc(max_made, 1)
                if cur.real():
                    q = cur.ring(2)
                    wait(dve, low1_made, cur)
                    wait(dve, l2_done, cur - 2)
                    leaky(y1[q], y1_ps, b1_sb, low1[q]).then_inc(y1_made, 1)
                if n1.real():
                    q = n1.ring(2)
                    dve.wait_ge(const_made, 8)
                    wait(dve, stats_made, n1)
                    wait(dve, nmr_made, n1 - 2)
                    for s in range(TG):
                        last = V.bn_aggr(mv[q][:, s, :], stats[:, q, s, :])
                    last.then_inc(mv_made, 1)
                    wait(dve, mv_made, n1)
                    V.tensor_scalar(var[1][q][:, :], mv[q][:, :, 1], EPS, None, op0=ALU.add).then_inc(var_made[1], 1)

            slots(dve, slot)

        @block.scalar
        def _(act):
            S = nc.scalar
            act.preload_act_table_set("natural_log_exp_and_others")
            act.wait_ge(w_loaded, 16 * 10)
            act.wait_ge(const_made, 8)
            act.wait_ge(setup_dve, 24)

            def root(j, g):
                q = g.ring(2)
                wait(act, var_made[j], g)
                S.activation(lnv[j][q][:, :], var[j][q][:, :], ACT.Ln).then_inc(ln_made[j], 1)

            def root_exp(j, g):
                q = g.ring(2)
                wait(act, ln_made[j], g)
                wait(act, rstd_made[j], g - 2)
                S.activation(y0[j][q][:, :], lnv[j][q][:, :], ACT.Exp, scale=-0.5).then_inc(y0_made[j], 1)

            def squares(g, tiles):
                q = g.ring(2)
                wait(act, z_done, g)
                wait(act, var_made[0], g - 2)
                for s in tiles:
                    wait(act, ssq_made, g - 2, TG)
                    S.activation(junk[:, q, s, :], z_ps[q][:, s, :], ACT.Square,
                                 accum_out=ssq[q][:, s:s + 1]).then_inc(ssq_made, 1)

            def slot(n):
                front, up, prev, back, n2 = n + 2, n + 1, n - 1, n - 2, n - 4
                if n2.real():
                    root(1, n2)
                if back.real():
                    squares(back, (0, 1))
                if n2.real():
                    root_exp(1, n2)
                if n.real():
                    q = n.ring(2)
                    wait(act, sx_done, n)
                    wait(act, z_done, n - 2)
                    S.activation(sx[q][:, :], sx_ps[:, :], ACT.Copy).then_inc(sx_made, 1)
                if back.real():
                    squares(back, (2,))
                if prev.real():
                    q = prev.ring(2)
                    wait(act, l2_done, prev)
                    wait(act, y2_made, prev - 2)
                    S.activation(low2[q][:, :], y2_ps[:, :], ACT.Identity, bias=b2_low[:, 0:1],
                                 scale=SLOPE).then_inc(low2_made, 1)
                if up.real():
                    q = up.ring(2)
                    wait(act, transposed, up)
                    wait(act, sx_done, up - 2)
                    for t in range(2):
                        at_t = slice(BLK * t, BLK * t + BLK)
                        S.activation(pT[q][at_t, :, t, :].rearrange("p (b h) i -> p h b i", b=2),
                                     pt_ps[q][at_t, 0:2 * P].rearrange("p (h b i) -> p h b i", h=2, b=2),
                                     ACT.Copy).then_inc(pT_made, 1)
                if n.real():
                    q = n.ring(2)
                    wait(act, l1_done, n)
                    wait(act, y1_made, n - 2)
                    S.activation(low1[q][:, :], y1_ps[:, :], ACT.Identity, bias=b1_low[:, 0:1],
                                 scale=SLOPE).then_inc(low1_made, 1)
                if back.real():
                    squares(back, (3,))
                    q = back.ring(2)
                    wait(act, ssq_made, back, TG)
                    S.activation(lnv[0][q][:, :], ssq[q][:, :], ACT.Ln, scale=1.0 / F, bias=eps[:, 0:1]).then_inc(ln_made[0], 1)
                if front.real():
                    q = front.ring(2)
                    wait(act, shifted, front)
                    wait(act, transposed, front - 2)
                    S.activation(prob[q][:, :, :], score[q][:, :, :], ACT.Exp).then_inc(exp_made, 1)
                if back.real():
                    root_exp(0, back)

            slots(act, slot)

        @block.tensor
        def _(pe):
            T = nc.tensor
            pe.wait_ge(w_loaded, 16 * 10)
            pe.wait_ge(const_made, 3)
            T.transpose(sx_ps[:, 0:P], W_sb[:, :], ident[:, :]).then_inc(setup_pe, 1)
            pe.wait_ge(setup_dve, 2)
            T.matmul(y1_ps[:, 0:F], a_wide[:, :], WT[:, :], start=True, stop=True).then_inc(setup_pe, 1)
            T.matmul(y2_ps[:, 0:F], WT[:, :], W1_sb[:, :], start=True, stop=True).then_inc(setup_pe, 1)

            def layer(out_ps, weights, rhs):
                return T.matmul(out_ps[:, :], weights[:, :], rhs[:, :], start=True, stop=True)

            def slot(n):
                up, prev = n + 1, n - 1
                if n.real():
                    q = n.ring(2)
                    wait(pe, pT_made, n, 2)
                    pe.wait_ge(x_loaded[n.ring(4)], n.dma_done())
                    wait(pe, sx_made, n - 1)
                    if isinstance(n.i, int) and n.k == 0:
                        pe.wait_ge(setup_dve, 22)
                    for s in range(TG):
                        last = T.matmul(sx_ps[:, s * P:(s + 1) * P], xt[n.ring(4)][:, s, :],
                                        pT[q][:, s, :, :].rearrange("p t i -> p (t i)"), start=True, stop=True)
                    last.then_inc(sx_done, 1)
                if prev.real():
                    wait(pe, y1_made, prev)
                    wait(pe, y2_made, prev - 1)
                    layer(y2_ps, W2_sb, y1[prev.ring(2)]).then_inc(l2_done, 1)
                if up.real():
                    q = up.ring(2)
                    wait(pe, prob_made, up)
                    wait(pe, pT_made, up - 2, 2)
                    for h in range(2):
                        last = T.transpose(pt_ps[q][:, h * P:(h + 1) * P],
                                           prob[q][:, 2 * h:2 * h + 2, :].rearrange("p t j -> p (t j)"), ident[:, :])
                    last.then_inc(transposed, 1)
                if n.real():
                    wait(pe, sx_made, n)
                    wait(pe, y1_made, n - 1)
                    layer(y1_ps, WW1, sx[n.ring(2)]).then_inc(l1_done, 1)
                if prev.real():
                    q = prev.ring(2)
                    wait(pe, t_made, prev - 2)
                    T.matmul(z_ps[q][:, :, :].rearrange("p s f -> p (s f)"), ones[:, :],
                             b3_rows[:, :, :].rearrange("p s f -> p (s f)"), start=True, stop=False)
                    for s in range(TG):
                        T.matmul(z_ps[q][:, s, :], sx[q][:, s * P:(s + 1) * P], Wc[:, :], start=False, stop=False)
                    wait(pe, y2_made, prev)
                    for s in range(TG):
                        last = T.matmul(z_ps[q][:, s, :], y2[q][:, s * P:(s + 1) * P], W3c[:, :], start=False,
                                        stop=s == TG - 1)
                    last.then_inc(z_done, 1)

            slots(pe, slot)


_NAMES = ["x", "adj"] + ["L0_gnn_" + n for n in ("W", "a", "ln_g", "ln_b", "W1", "b1", "W2", "b2", "W3", "b3")]


def kernel(**inputs):
    import numpy as np
    import concourse.bacc as bacc
    from concourse.bass_utils import run_bass_kernel_spmd

    nc = bacc.Bacc("TRN2", target_bir_lowering=False, num_devices=1)
    arrays, args = {}, []
    for name in _NAMES:
        array = np.ascontiguousarray(inputs[name])
        arrays[f"in_{name}"] = array
        args.append(nc.dram_tensor(f"in_{name}", array.shape, mybir.dt.from_np(array.dtype), kind="ExternalInput").ap())
    args.append(nc.dram_tensor("out", (B, N, F), mybir.dt.float32, kind="ExternalOutput").ap())
    program(nc, *args)
    done = run_bass_kernel_spmd(nc, [arrays], core_ids=[0])
    return done.results[0]["out"]
```

```python
import concourse.bass as bass
from concourse import mybir
from contextlib import ExitStack

B, N, F, BLK = 8, 2048, 128, 64
P = 128
TG = 4
ROWS = TG * P
GROUPS = B * N // ROWS
GPB = N // ROWS
BG = ROWS // BLK
EPS = 1e-5
SLOPE_E, SLOPE = 0.2, 0.01
FIRST, LAST = -3, GROUPS + 3
LOOP_FROM, LOOP_TO = 5, 29


class Group:

    def __init__(self, i, k):
        self.i, self.k = i, k

    def __add__(self, d):
        return Group(self.i, self.k + d)

    def __sub__(self, d):
        return Group(self.i, self.k - d)

    def real(self):
        return not isinstance(self.i, int) or 0 <= 4 * self.i + self.k < GROUPS

    def ring(self, size):
        return self.k % size

    def batch(self):
        return self.i + self.k // GPB

    def done(self, per=1):
        return self.i * (4 * per) + (self.k + 1) * per

    def dma_done(self, dmas=1):
        return (self.i + self.k // 4 + 1) * (16 * dmas)


def wait(eng, sem, group, per=1):
    if isinstance(group.i, int) and group.done(per) <= 0:
        return
    eng.wait_ge(sem, group.done(per))


def slots(eng, slot, late=0):
    for n in range(FIRST, LOOP_FROM - late):
        slot(Group(0, n))
    with eng.Fori(LOOP_FROM // 4, LOOP_TO // 4) as i:
        for k in range(4):
            slot(Group(i, LOOP_FROM % 4 + k - late))
    for n in range(LOOP_TO - late, LAST + 1):
        slot(Group(0, n))


def program(nc, x, adj, W, a, ln_g, ln_b, W1, b1, W2, b2, W3, b3, out):
    f32, bf16 = mybir.dt.float32, mybir.dt.bfloat16
    ALU, ACT, AX = mybir.AluOpType, mybir.ActivationFunctionType, mybir.AxisListType

    ctx = ExitStack()
    with ctx:
        def sb(name, shape, dt=f32):
            return ctx.enter_context(nc.sbuf_tensor(name, shape, dt))

        def ps(name, shape, dt=f32):
            return ctx.enter_context(nc.psum_tensor(name, shape, dt))

        def sem(name):
            return ctx.enter_context(nc.semaphore(name))

        W_sb, W1_sb, W2_sb, W3_sb = (sb(f"{n}_sb", [P, F]) for n in ("W", "W1", "W2", "W3"))
        a_sb, b1_sb, b2_sb = (sb(f"{n}_sb", [P, 1]) for n in ("a", "b1", "b2"))
        g_bc, b_bc, b3_bc = (sb(f"{n}_bc", [P, F]) for n in ("g", "b", "b3"))
        WT = sb("WT", [P, F])
        WW1 = sb("WW1", [P, F])
        W2T, W23 = sb("W2T", [P, F]), sb("W23", [P, F])
        wa_bc = sb("wa_bc", [P, F])
        a_wide = sb("a_wide", [P, P])
        Wc, W3c, b3c = sb("Wc", [P, F]), sb("W3c", [P, F]), sb("b3c", [P, F])
        wmean = sb("wmean", [P, 3])
        ident = sb("ident", [P, P])
        ones_f = sb("ones_f", [P, P])
        ones = sb("ones", [P, P], bf16)
        b3_hi, b3_mid, b3_lo = (sb(f"b3_{n}", [P, F], bf16) for n in ("hi", "mid", "lo"))
        b3_rest, b3_rest2 = sb("b3_rest", [P, F]), sb("b3_rest2", [P, F])
        b3_rows = sb("b3_rows", [P, TG, F], bf16)
        b3_sel = sb("b3_sel", [P, F])
        b3_sel2 = sb("b3_sel2", [P, F])
        eps = sb("eps", [P, 1])

        xt = [sb(f"x{i}", [P, TG, F]) for i in range(4)]
        at = [sb(f"adj{i}", [P, TG, BLK]) for i in range(4)]
        xw = [sb(f"xw{i}", [P, TG, F]) for i in range(2)]
        e_x = [sb(f"e_x{i}", [P, TG]) for i in range(2)]
        e_lk = [sb(f"e_lk{i}", [P, TG]) for i in range(2)]
        score = [sb(f"score{i}", [P, TG, BLK]) for i in range(2)]
        smax = [sb(f"smax{i}", [P, TG]) for i in range(2)]
        prob = [sb(f"prob{i}", [P, TG, BLK]) for i in range(2)]
        psum_ = [sb(f"probsum{i}", [P, TG]) for i in range(2)]
        pinv = [sb(f"probinv{i}", [P, TG]) for i in range(2)]
        pT = [sb(f"pT{i}", [P, TG, 2, BLK]) for i in range(2)]
        sx = [sb(f"sx{i}", [P, ROWS]) for i in range(2)]
        y1 = [sb(f"y1_{i}", [P, ROWS]) for i in range(2)]
        y2 = [sb(f"y2_{i}", [P, ROWS]) for i in range(2)]
        up1 = [sb(f"up1_{i}", [P, ROWS]) for i in range(2)]
        b1_up, b2_up = sb("b1_up", [P, 1]), sb("b2_up", [P, 1])
        b1_s, b2_s, b2_all, b2_wide = sb("b1_s", [P, 1]), sb("b2_s", [P, 1]), sb("b2_all", [P, 1]), sb("b2_wide", [P, P])
        junk = sb("junk", [P, 2, TG, F])
        ssq = [sb(f"ssq{i}", [P, TG]) for i in range(2)]
        u = [sb(f"u{i}", [P, TG, F]) for i in range(4)]
        t1 = [sb(f"t{i}", [P, TG, F]) for i in range(2)]
        r = [sb(f"r{i}", [P, TG, F]) for i in range(2)]
        stats = sb("stats", [P, 2, TG, 6])
        mv = [sb(f"mv{i}", [P, TG, 2]) for i in range(2)]
        o = [sb(f"o{i}", [P, TG, F]) for i in range(4)]
        small = lambda n: [[sb(f"{n}{j}{i}", [P, TG]) for i in range(2)] for j in range(2)]
        var, lnv, y0, y0sq, corr, rstd = (small(n) for n in ("var", "lnv", "y0_", "y0sq", "corr", "rstd"))
        nmr = [sb(f"nmr{i}", [P, TG]) for i in range(2)]

        pt_ps = [ps(f"pt_ps{i}", [P, 512]) for i in range(2)]
        sx_ps, y1_ps, y2_ps = ps("sx_ps", [P, 512]), ps("y1_ps", [P, 512]), ps("y2_ps", [P, 512])
        z_ps = [ps(f"z_ps{i}", [P, TG, F]) for i in range(2)]

        w_loaded = sem("w_loaded")
        const_made = sem("const_made")
        setup_pe = sem("setup_pe")
        setup_dve = sem("setup_dve")
        setup_w2 = sem("setup_w2")
        x_loaded = [sem(f"x_loaded{i}") for i in range(4)]
        adj_loaded = [sem(f"adj_loaded{i}") for i in range(4)]
        stored = [sem(f"stored{i}") for i in range(4)]
        xw_made = sem("xw_made")
        e_summed = sem("e_summed")
        e_made = sem("e_made")
        scaled = sem("scaled")
        max_made = sem("max_made")
        shifted = sem("shifted")
        exp_made = sem("exp_made")
        sum_made = sem("sum_made")
        inv_made = sem("inv_made")
        prob_made = sem("prob_made")
        transposed = sem("transposed")
        pT_made = sem("pT_made")
        sx_done = sem("sx_done")
        sx_made = sem("sx_made")
        l1_done = sem("l1_done")
        up1_made = sem("up1_made")
        y1_made = sem("y1_made")
        l2_done = sem("l2_done")
        y2_made = sem("y2_made")
        z_done = sem("z_done")
        ssq_made = sem("ssq_made")
        u_made = sem("u_made")
        t_made = sem("t_made")
        r_made = sem("r_made")
        stats_made = sem("stats_made")
        mv_made = sem("mv_made")
        var_made, ln_made, y0_made, sq_made, corr_made, rstd_made = (
            [sem(f"{n}{j}") for j in range(2)]
            for n in ("var_made", "ln_made", "y0_made", "sq_made", "corr_made", "rstd_made"))
        nmr_made = sem("nmr_made")
        o_made = sem("o_made")

        x_flat = x.rearrange("b n f -> (b n) f")
        out_flat = out.rearrange("b n f -> (b n) f")

        def rows_of(flat, g):
            return bass.AP(tensor=flat.tensor, offset=g.i * (4 * ROWS * F) + g.k * (ROWS * F),
                           ap=[[F, P], [P * F, TG], [1, F]])

        def blocks_of(g, t):
            step = BLK * (N + 1)
            return bass.AP(tensor=adj.tensor, offset=g.batch() * (N * N) + ((g.k % GPB) * BG + t) * step,
                           ap=[[N, BLK], [2 * step, TG], [1, BLK]])

        def wide(v):
            return v[:, :].rearrange("p (s o) -> p s o", o=1).broadcast_to([P, TG, BLK])

        def each_tile(v):
            return v[:, :].rearrange("p (o f) -> p o f", o=1).broadcast_to([P, TG, F])

        block = ctx.enter_context(nc.Block())

        @block.sync
        def _(sync):
            def load(g):
                if not g.real():
                    return
                wait(sync, sx_done, g - 4)
                wait(sync, u_made, g - 4)
                sync.dma_start(xt[g.ring(4)][:, :, :], rows_of(x_flat, g)).then_inc(x_loaded[g.ring(4)], 16)
                wait(sync, scaled, g - 4)
                for t in range(2):
                    sync.dma_start(at[g.ring(4)][BLK * t:BLK * t + BLK, :, :],
                                   blocks_of(g, t)).then_inc(adj_loaded[g.ring(4)], 16)

            def slot(n):
                load(n + 4)
                g = n - 4
                if g.real():
                    wait(sync, o_made, g)
                    sync.dma_start(rows_of(out_flat, g), o[g.ring(4)][:, :, :]).then_inc(stored[g.ring(4)], 16)

            load(Group(0, 0))
            weights = [(W_sb, W), (a_sb, a), (W1_sb, W1), (W3_sb, W3), (W2_sb, W2)]
            for dst, src in weights:
                sync.dma_start(dst[:, :], src[:, :]).then_inc(w_loaded, 16)
            for dst, src in ((b1_sb, b1), (b2_sb, b2)):
                sync.dma_start(dst[:, :], src.rearrange("(p o) -> p o", o=1)).then_inc(w_loaded, 16)
            for dst, src in ((g_bc, ln_g), (b_bc, ln_b), (b3_bc, b3)):
                sync.dma_start(dst[:, :], src.rearrange("(o f) -> o f", o=1).broadcast_to([P, F])).then_inc(w_loaded, 16)
            slots(sync, slot, late=1)
            for k in range(4):
                sync.wait_ge(stored[k], 16 * (GROUPS // 4))

        @block.gpsimd
        def _(pool):
            pool.memset(ident[:, :], 0.0).then_inc(const_made, 1)
            pool.memset(ones_f[:, :], 1.0).then_inc(const_made, 1)
            pool.wait_ge(const_made, 1)
            pool.affine_select(out=ident[:, :], in_=ident[:, :], compare_op=ALU.not_equal, fill=1.0,
                               base=0, pattern=[[-1, P]], channel_multiplier=1).then_inc(const_made, 1)
            pool.memset(ones[:, :], 1.0).then_inc(const_made, 1)
            pool.memset(eps[:, :], EPS).then_inc(const_made, 1)
            pool.memset(b3_rows[:, :, :], 0.0).then_inc(const_made, 1)
            for i in range(2):
                pool.memset(pT[i][:, :, :, :], 0.0).then_inc(const_made, 1)
            pool.wait_ge(setup_dve, 3)

            def slot(n):
                g = n - 4
                if g.real():
                    wait(pool, r_made, g)
                    if not isinstance(g.i, int) or g.k >= 4:
                        pool.wait_ge(stored[g.ring(4)], (g - 4).dma_done())
                g = n + 1
                if g.real():
                    wait(pool, inv_made, g)
                    wait(pool, exp_made, g)
                    pool.tensor_tensor(prob[g.ring(2)][:, :, :], prob[g.ring(2)][:, :, :],
                                       wide(pinv[g.ring(2)]), ALU.mult).then_inc(prob_made, 1)
                g = n + 2
                if g.real():
                    pool.wait_ge(adj_loaded[g.ring(4)], g.dma_done(2))
                    wait(pool, e_made, g)
                    wait(pool, exp_made, g - 2)
                    pool.tensor_tensor(score[g.ring(2)][:, :, :], at[g.ring(4)][:, :, :],
                                       wide(e_lk[g.ring(2)]), ALU.mult).then_inc(scaled, 1)
                g = n + 3
                if g.real():
                    pool.wait_ge(x_loaded[g.ring(4)], g.dma_done())
                    wait(pool, e_summed, g - 2)
                    pool.tensor_tensor(xw[g.ring(2)][:, :, :], xt[g.ring(4)][:, :, :], each_tile(wa_bc),
                                       ALU.mult).then_inc(xw_made, 1)
                g = n + 2
                if g.real():
                    wait(pool, max_made, g)
                    wait(pool, scaled, g)
                    pool.tensor_tensor(score[g.ring(2)][:, :, :], score[g.ring(2)][:, :, :],
                                       wide(smax[g.ring(2)]), ALU.subtract).then_inc(shifted, 1)
                g = n - 4
                if g.real():
                    pool.wait_ge(const_made, 8)
                    wait(pool, rstd_made[1], g)
                    wait(pool, nmr_made, g)
                    for s in range(TG):
                        last = pool.tensor_scalar(o[g.ring(4)][:, s, :], r[g.ring(2)][:, s, :],
                                                  rstd[1][g.ring(2)][:, s:s + 1], nmr[g.ring(2)][:, s:s + 1],
                                                  op0=ALU.mult, op1=ALU.add)
                    last.then_inc(o_made, 1)

            slots(pool, slot)

        @block.vector
        def _(dve):
            dve.wait_ge(w_loaded, 16 * 10)
            dve.wait_ge(const_made, 8)
            V = nc.vector
            V.tensor_scalar(a_wide[:, :], ones_f[:, :], a_sb[:, 0:1], None, op0=ALU.mult).then_inc(setup_dve, 1)
            dve.wait_ge(setup_pe, 1)
            V.tensor_copy(WT[:, :], sx_ps[:, 0:P]).then_inc(setup_dve, 1)
            V.tensor_copy(W2T[:, :], sx_ps[:, P:2 * P]).then_inc(setup_w2, 1)
            dve.wait_ge(setup_pe, 2)
            V.tensor_copy(wa_bc[:, :], y1_ps[:, 0:F]).then_inc(setup_dve, 1)
            dve.wait_ge(setup_pe, 3)
            V.tensor_copy(WW1[:, :], y2_ps[:, 0:F]).then_inc(setup_dve, 1)
            done = 4
            for j, (src, dst) in enumerate(((W_sb, Wc), (W3_sb, W3c), (b3_bc, b3c))):
                V.tensor_reduce(wmean[:, j:j + 1], src[:, :], op=ALU.add, axis=AX.X).then_inc(setup_dve, 1)
                dve.wait_ge(setup_dve, done + 1)
                V.tensor_scalar(wmean[:, j:j + 1], wmean[:, j:j + 1], 1.0 / F, None, op0=ALU.mult).then_inc(setup_dve, 1)
                dve.wait_ge(setup_dve, done + 2)
                V.tensor_scalar(dst[:, :], src[:, :], wmean[:, j:j + 1], None, op0=ALU.subtract).then_inc(setup_dve, 1)
                done += 3
            def then(instruction):
                nonlocal done
                instruction.then_inc(setup_dve, 1)
                done += 1
                dve.wait_ge(setup_dve, done)

            then(V.tensor_scalar(b1_up[:, :], b1_sb[:, :], 1 - SLOPE, None, op0=ALU.mult))
            then(V.tensor_scalar(b1_s[:, :], b1_sb[:, :], SLOPE, None, op0=ALU.mult))
            dve.wait_ge(setup_pe, 4)
            then(V.tensor_tensor(b2_all[:, :], b2_sb[:, :], y1_ps[:, F:F + 1], ALU.add))
            then(V.tensor_scalar(b2_up[:, :], b2_all[:, :], 1 - SLOPE, None, op0=ALU.mult))
            then(V.tensor_scalar(b2_s[:, :], b2_all[:, :], SLOPE, None, op0=ALU.mult))
            then(V.tensor_scalar(b2_wide[:, :], ones_f[:, :], b2_s[:, 0:1], None, op0=ALU.mult))
            dve.wait_ge(setup_pe, 5)
            then(V.tensor_tensor(b3c[:, :], b3c[:, :], y2_ps[:, F:2 * F], ALU.add))
            then(V.tensor_copy(b3_hi[:, :], b3c[:, :]))
            then(V.tensor_tensor(b3_rest[:, :], b3c[:, :], b3_hi[:, :], ALU.subtract))
            then(V.tensor_copy(b3_mid[:, :], b3_rest[:, :]))
            then(V.tensor_tensor(b3_rest2[:, :], b3_rest[:, :], b3_mid[:, :], ALU.subtract))
            then(V.tensor_copy(b3_lo[:, :], b3_rest2[:, :]))
            then(V.tensor_scalar(b3_sel[:, :], b3_hi[:, :], ident[:, 0:1], None, op0=ALU.mult))
            then(V.scalar_tensor_tensor(b3_sel2[:, :], b3_mid[:, :], ident[:, 1:2], b3_sel[:, :], op0=ALU.mult, op1=ALU.add))
            then(V.scalar_tensor_tensor(b3_sel[:, :], b3_lo[:, :], ident[:, 2:3], b3_sel2[:, :], op0=ALU.mult, op1=ALU.add))
            V.tensor_copy(b3_rows[:, :, :], each_tile(b3_sel)).then_inc(setup_dve, 1)
            dve.wait_ge(setup_pe, 6)
            V.tensor_scalar(W23[:, :], z_ps[0][:, 0, :], SLOPE, None, op0=ALU.mult).then_inc(setup_dve, 1)
            def newton(j, g, step):
                q = g.ring(2)
                if step == 0:
                    wait(dve, y0_made[j], g)
                    V.tensor_tensor(y0sq[j][q][:, :], y0[j][q][:, :], y0[j][q][:, :], ALU.mult).then_inc(sq_made[j], 1)
                elif step == 1:
                    wait(dve, sq_made[j], g)
                    V.scalar_tensor_tensor(corr[j][q][:, :], y0sq[j][q][:, :], -0.5, var[j][q][:, :],
                                           op0=ALU.mult, op1=ALU.mult).then_inc(corr_made[j], 1)
                else:
                    wait(dve, corr_made[j], g)
                    V.scalar_tensor_tensor(rstd[j][q][:, :], corr[j][q][:, :], 1.5, y0[j][q][:, :],
                                           op0=ALU.add, op1=ALU.mult).then_inc(rstd_made[j], 1)

            def slot(n):
                up, front, ahead = n + 1, n + 2, n + 3
                n2, n3, n4 = n - 2, n - 3, n - 4
                if up.real():
                    q = up.ring(2)
                    wait(dve, exp_made, up)
                    V.tensor_reduce(psum_[q][:, :], prob[q][:, :, :], op=ALU.add, axis=AX.X).then_inc(sum_made, 1)
                if n4.real():
                    newton(1, n4, 0)
                if up.real():
                    q = up.ring(2)
                    wait(dve, sum_made, up)
                    V.reciprocal(pinv[q][:, :], psum_[q][:, :]).then_inc(inv_made, 1)
                if n3.real():
                    q = n3.ring(2)
                    wait(dve, rstd_made[0], n3)
                    wait(dve, r_made, n3 - 2)
                    for s in range(TG):
                        last = V.scalar_tensor_tensor(t1[q][:, s, :], z_ps[q][:, s, :], rstd[0][q][:, s:s + 1],
                                                      g_bc[:, :], op0=ALU.mult, op1=ALU.mult)
                    last.then_inc(t_made, 1)
                if n4.real():
                    newton(1, n4, 1)
                if front.real():
                    q = front.ring(2)
                    wait(dve, scaled, front)
                    wait(dve, shifted, front - 2)
                    V.tensor_reduce(smax[q][:, :], score[q][:, :, :], op=ALU.max, axis=AX.X).then_inc(max_made, 1)
                if n4.real():
                    newton(1, n4, 2)
                if n3.real():
                    q = n3.ring(2)
                    wait(dve, t_made, n3)
                    wait(dve, u_made, n3)
                    wait(dve, o_made, n3 - 2)
                    V.tensor_tensor(r[q][:, :, :], t1[q][:, :, :], u[n3.ring(4)][:, :, :], ALU.add).then_inc(r_made, 1)
                if n4.real():
                    q = n4.ring(2)
                    wait(dve, rstd_made[1], n4)
                    V.scalar_tensor_tensor(nmr[q][:, :], mv[q][:, :, 0], -1.0, rstd[1][q][:, :],
                                           op0=ALU.mult, op1=ALU.mult).then_inc(nmr_made, 1)
                if n3.real():
                    q = n3.ring(2)
                    wait(dve, r_made, n3)
                    wait(dve, mv_made, n3 - 2)
                    for s in range(TG):
                        last = V.bn_stats(stats[:, q, s, :], r[q][:, s, :])
                    last.then_inc(stats_made, 1)
                if n2.real():
                    q = n2.ring(2)
                    wait(dve, ssq_made, n2, TG)
                    V.tensor_scalar(var[0][q][:, :], ssq[q][:, :], 1.0 / F, EPS, op0=ALU.mult,
                                    op1=ALU.add).then_inc(var_made[0], 1)
                if n.real():
                    q = n.ring(2)
                    wait(dve, up1_made, n)
                    wait(dve, z_done, n - 2)
                    V.scalar_tensor_tensor(y1[q][:, :], y1_ps[:, :], SLOPE, up1[q][:, :],
                                           op0=ALU.mult, op1=ALU.add).then_inc(y1_made, 1)
                if n3.real():
                    q = n3.ring(2)
                    dve.wait_ge(const_made, 8)
                    wait(dve, stats_made, n3)
                    wait(dve, nmr_made, n3 - 2)
                    for s in range(TG):
                        last = V.bn_aggr(mv[q][:, s, :], stats[:, q, s, :])
                    last.then_inc(mv_made, 1)
                if n2.real():
                    newton(0, n2, 0)
                if n3.real():
                    q = n3.ring(2)
                    wait(dve, mv_made, n3)
                    V.tensor_scalar(var[1][q][:, :], mv[q][:, :, 1], EPS, None, op0=ALU.add).then_inc(var_made[1], 1)
                if n2.real():
                    wait(dve, var_made[0], n2)
                    newton(0, n2, 1)
                if up.real():
                    dve.wait_ge(x_loaded[up.ring(4)], up.dma_done())
                    wait(dve, r_made, up - 4)
                    V.tensor_tensor(u[up.ring(4)][:, :, :], xt[up.ring(4)][:, :, :], each_tile(b_bc),
                                    ALU.add).then_inc(u_made, 1)
                if n2.real():
                    newton(0, n2, 2)
                if ahead.real():
                    q = ahead.ring(2)
                    wait(dve, e_summed, ahead)
                    wait(dve, scaled, ahead - 2)
                    V.scalar_tensor_tensor(e_lk[q][:, :], e_x[q][:, :], SLOPE_E, e_x[q][:, :],
                                           op0=ALU.mult, op1=ALU.max).then_inc(e_made, 1)

            slots(dve, slot)

        @block.scalar
        def _(act):
            S = nc.scalar
            act.preload_act_table_set("natural_log_exp_and_others")
            act.wait_ge(w_loaded, 16 * 10)
            act.wait_ge(const_made, 8)
            act.wait_ge(setup_dve, 19)

            def root(j, g):
                q = g.ring(2)
                wait(act, var_made[j], g)
                S.activation(lnv[j][q][:, :], var[j][q][:, :], ACT.Ln).then_inc(ln_made[j], 1)

            def root_exp(j, g):
                q = g.ring(2)
                wait(act, ln_made[j], g)
                if j == 0:
                    wait(act, rstd_made[j], g - 2)
                S.activation(y0[j][q][:, :], lnv[j][q][:, :], ACT.Exp, scale=-0.5).then_inc(y0_made[j], 1)

            def squares(g, tiles):
                q = g.ring(2)
                wait(act, z_done, g)
                wait(act, var_made[0], g - 2)
                for s in tiles:
                    wait(act, ssq_made, g - 2, TG)
                    S.activation(junk[:, q, s, :], z_ps[q][:, s, :], ACT.Square,
                                 accum_out=ssq[q][:, s:s + 1]).then_inc(ssq_made, 1)

            def slot(n):
                front, up, ahead, prev, n2, n3 = n + 2, n + 1, n + 3, n - 1, n - 2, n - 3
                if n2.real():
                    squares(n2, (0, 1, 2))
                if n.real():
                    q = n.ring(2)
                    wait(act, sx_done, n)
                    wait(act, z_done, n - 2)
                    S.activation(sx[q][:, :], sx_ps[:, :], ACT.Copy).then_inc(sx_made, 1)
                if n2.real():
                    squares(n2, (3,))
                    q = n2.ring(2)
                    wait(act, ssq_made, n2, TG)
                    S.activation(lnv[0][q][:, :], ssq[q][:, :], ACT.Ln, scale=1.0 / F, bias=eps[:, 0:1]).then_inc(ln_made[0], 1)
                if prev.real():
                    q = prev.ring(2)
                    wait(act, l2_done, prev)
                    wait(act, z_done, prev - 2)
                    S.activation(y2[q][:, :], y2_ps[:, :], ACT.Relu, bias=b2_up[:, 0:1],
                                 scale=1 - SLOPE).then_inc(y2_made, 1)
                if n.real():
                    q = n.ring(2)
                    wait(act, l1_done, n)
                    wait(act, y1_made, n - 2)
                    S.activation(up1[q][:, :], y1_ps[:, :], ACT.Relu, bias=b1_up[:, 0:1],
                                 scale=1 - SLOPE).then_inc(up1_made, 1)
                if n2.real():
                    root_exp(0, n2)
                if up.real():
                    q = up.ring(2)
                    wait(act, transposed, up)
                    wait(act, sx_done, up - 2)
                    for half in range(2):
                        for t in range(2):
                            last = S.activation(
                                pT[q][BLK * t:BLK * t + BLK, half:TG:2, t, :],
                                pt_ps[q][BLK * half:BLK * half + BLK, 0:2 * P].rearrange(
                                    "p (h t i) -> p h t i", h=2, t=2)[:, :, t, :], ACT.Copy)
                    last.then_inc(pT_made, 1)
                ahead = n + 3
                if ahead.real():
                    q = ahead.ring(2)
                    wait(act, xw_made, ahead)
                    wait(act, e_made, ahead - 2)
                    for s in range(TG):
                        last = S.activation(xw[q][:, s, :], xw[q][:, s, :], ACT.Identity, accum_out=e_x[q][:, s:s + 1])
                    last.then_inc(e_summed, 1)
                if front.real():
                    q = front.ring(2)
                    wait(act, shifted, front)
                    wait(act, transposed, front - 2)
                    S.activation(prob[q][:, :, :], score[q][:, :, :], ACT.Exp).then_inc(exp_made, 1)
                if n3.real():
                    root(1, n3)
                    root_exp(1, n3)

            slots(act, slot)

        @block.tensor
        def _(pe):
            T = nc.tensor
            pe.wait_ge(w_loaded, 16 * 10)
            pe.wait_ge(const_made, 3)
            T.transpose(sx_ps[:, 0:P], W_sb[:, :], ident[:, :])
            T.transpose(sx_ps[:, P:2 * P], W2_sb[:, :], ident[:, :]).then_inc(setup_pe, 1)
            pe.wait_ge(setup_dve, 2)
            T.matmul(y1_ps[:, 0:F], a_wide[:, :], WT[:, :], start=True, stop=True).then_inc(setup_pe, 1)
            T.matmul(y2_ps[:, 0:F], WT[:, :], W1_sb[:, :], start=True, stop=True).then_inc(setup_pe, 1)

            pe.wait_ge(setup_dve, 15)
            T.matmul(y1_ps[:, F:F + 1], W2_sb[:, :], b1_s[:, :], start=True, stop=True).then_inc(setup_pe, 1)
            pe.wait_ge(setup_dve, 19)
            T.matmul(y2_ps[:, F:2 * F], b2_wide[:, :], W3c[:, :], start=True, stop=True).then_inc(setup_pe, 1)
            pe.wait_ge(setup_w2, 1)
            T.matmul(z_ps[0][:, 0, :], W2T[:, :], W3c[:, :], start=True, stop=True).then_inc(setup_pe, 1)

            def layer(out_ps, weights, rhs):
                return T.matmul(out_ps[:, :], weights[:, :], rhs[:, :], start=True, stop=True)

            def slot(n):
                up, prev = n + 1, n - 1
                if n.real():
                    q = n.ring(2)
                    wait(pe, pT_made, n)
                    pe.wait_ge(x_loaded[n.ring(4)], n.dma_done())
                    wait(pe, sx_made, n - 1)
                    if isinstance(n.i, int) and n.k == 0:
                        pe.wait_ge(setup_dve, 30)
                    for s in range(TG):
                        last = T.matmul(sx_ps[:, s * P:(s + 1) * P], xt[n.ring(4)][:, s, :],
                                        pT[q][:, s, :, :].rearrange("p t i -> p (t i)"), start=True, stop=True)
                    last.then_inc(sx_done, 1)
                if prev.real():
                    wait(pe, y1_made, prev)
                    wait(pe, y2_made, prev - 1)
                    layer(y2_ps, W2_sb, y1[prev.ring(2)]).then_inc(l2_done, 1)
                if n.real():
                    wait(pe, sx_made, n)
                    wait(pe, y1_made, n - 1)
                    layer(y1_ps, WW1, sx[n.ring(2)]).then_inc(l1_done, 1)
                if up.real():
                    q = up.ring(2)
                    wait(pe, prob_made, up)
                    wait(pe, pT_made, up - 2)
                    for h in range(2):
                        last = T.transpose(pt_ps[q][:, h * P:(h + 1) * P],
                                           prob[q][:, 2 * h:2 * h + 2, :].rearrange("p t j -> p (t j)"), ident[:, :])
                    last.then_inc(transposed, 1)
                if prev.real():
                    q = prev.ring(2)
                    wait(pe, t_made, prev - 2)
                    T.matmul(z_ps[q][:, :, :].rearrange("p s f -> p (s f)"), ones[:, :],
                             b3_rows[:, :, :].rearrange("p s f -> p (s f)"), start=True, stop=False)
                    for s in range(TG):
                        T.matmul(z_ps[q][:, s, :], sx[q][:, s * P:(s + 1) * P], Wc[:, :], start=False, stop=False)
                    for s in range(TG):
                        T.matmul(z_ps[q][:, s, :], y1[q][:, s * P:(s + 1) * P], W23[:, :], start=False, stop=False)
                    wait(pe, y2_made, prev)
                    for s in range(TG):
                        last = T.matmul(z_ps[q][:, s, :], y2[q][:, s * P:(s + 1) * P], W3c[:, :], start=False,
                                        stop=s == TG - 1)
                    last.then_inc(z_done, 1)

            slots(pe, slot)


_NAMES = ["x", "adj"] + ["L0_gnn_" + n for n in ("W", "a", "ln_g", "ln_b", "W1", "b1", "W2", "b2", "W3", "b3")]


def kernel(**inputs):
    import numpy as np
    import concourse.bacc as bacc
    from concourse.bass_utils import run_bass_kernel_spmd

    nc = bacc.Bacc("TRN2", target_bir_lowering=False, num_devices=1)
    arrays, args = {}, []
    for name in _NAMES:
        array = np.ascontiguousarray(inputs[name])
        arrays[f"in_{name}"] = array
        args.append(nc.dram_tensor(f"in_{name}", array.shape, mybir.dt.from_np(array.dtype), kind="ExternalInput").ap())
    args.append(nc.dram_tensor("out", (B, N, F), mybir.dt.float32, kind="ExternalOutput").ap())
    program(nc, *args)
    done = run_bass_kernel_spmd(nc, [arrays], core_ids=[0])
    return done.results[0]["out"]
```

```python
import concourse.bass as bass
from concourse import mybir
from contextlib import ExitStack

B, N, F, BLK = 8, 2048, 128, 64
P = 128
TG = 4
ROWS = TG * P
GROUPS = B * N // ROWS
GPB = N // ROWS
BG = ROWS // BLK
EPS = 1e-5
SLOPE_E, SLOPE = 0.2, 0.01
FROM, LAST = 1, GROUPS + 3
LOOP_FROM, LOOP_TO = 5, 29


class Group:

    def __init__(self, i, k):
        self.i, self.k = i, k

    def __add__(self, d):
        return Group(self.i, self.k + d)

    def __sub__(self, d):
        return Group(self.i, self.k - d)

    def real(self):
        return not isinstance(self.i, int) or 0 <= 4 * self.i + self.k < GROUPS

    def last(self, back=0):
        return isinstance(self.i, int) and self.k == GROUPS - 1 - back

    def pair_real(self):
        return not isinstance(self.i, int) or 0 <= 4 * self.i + self.k <= GROUPS

    def norms(self):
        inner = not isinstance(self.i, int)
        return 0 if inner or self.k < GROUPS else 1, 2 if inner or self.k > 0 else 1

    def ring(self, size):
        return self.k % size

    def batch(self):
        return self.i + self.k // GPB

    def done(self):
        return self.i * 4 + (self.k + 1)

    def dma_done(self, dmas=1):
        return (self.i + self.k // 4 + 1) * (16 * dmas)


def wait(eng, sem, group):
    if isinstance(group.i, int) and group.done() <= 0:
        return
    eng.wait_ge(sem, group.done())


def slots(eng, slot, late=0, last=LAST):
    for n in range(FROM, LOOP_FROM - late):
        slot(Group(0, n))
    with eng.Fori(LOOP_FROM // 4, LOOP_TO // 4) as i:
        for k in range(4):
            slot(Group(i, LOOP_FROM % 4 + k - late))
    for n in range(LOOP_TO - late, last + 1):
        slot(Group(0, n))


def program(nc, x, adj, W, a, ln_g, ln_b, W1, b1, W2, b2, W3, b3, out):
    f32, bf16 = mybir.dt.float32, mybir.dt.bfloat16
    ALU, ACT, AX = mybir.AluOpType, mybir.ActivationFunctionType, mybir.AxisListType

    ctx = ExitStack()
    with ctx:
        def sb(name, shape, dt=f32):
            return ctx.enter_context(nc.sbuf_tensor(name, shape, dt))

        def ps(name, shape, dt=f32):
            return ctx.enter_context(nc.psum_tensor(name, shape, dt))

        def sem(name):
            return ctx.enter_context(nc.semaphore(name))

        W_sb, W1_sb, W2_sb, W3_sb = (sb(f"{n}_sb", [P, F]) for n in ("W", "W1", "W2", "W3"))
        a_sb, b1_sb, b2_sb = (sb(f"{n}_sb", [P, 1]) for n in ("a", "b1", "b2"))
        g_bc, b_bc, b3_bc = (sb(f"{n}_bc", [P, F]) for n in ("g", "b", "b3"))
        WT = sb("WT", [P, F])
        WW1 = sb("WW1", [P, F])
        W2T, W23 = sb("W2T", [P, F]), sb("W23", [P, F])
        wa_bc = sb("wa_bc", [P, F])
        a_wide = sb("a_wide", [P, P])
        Wc, W3c, b3c = sb("Wc", [P, F]), sb("W3c", [P, F]), sb("b3c", [P, F])
        wmean = sb("wmean", [P, 4])
        ident = sb("ident", [P, P])
        ones_f = sb("ones_f", [P, P])
        ones = sb("ones", [P, P], bf16)
        b3_hi, b3_mid = (sb(f"b3_{n}", [P, F], bf16) for n in ("hi", "mid"))
        b3_rest, b3_rest2, b3_all = sb("b3_rest", [P, F]), sb("b3_rest2", [P, F]), sb("b3_all", [P, F])
        b3_rows = sb("b3_rows", [P, F], bf16)
        W3_copy = sb("W3_copy", [P, F])

        xt = [sb(f"x{i}", [P, TG, F]) for i in range(4)]
        at = [sb(f"adj{i}", [P, TG, BLK]) for i in range(4)]
        xw = [sb(f"xw{i}", [P, TG, F]) for i in range(2)]
        e_x = [sb(f"e_x{i}", [P, TG]) for i in range(2)]
        e_lk = [sb(f"e_lk{i}", [P, TG]) for i in range(2)]
        score = [sb(f"score{i}", [P, TG, BLK]) for i in range(2)]
        smax = [sb(f"smax{i}", [P, TG]) for i in range(2)]
        prob = [sb(f"prob{i}", [P, TG, BLK]) for i in range(2)]
        psum_ = [sb(f"probsum{i}", [P, TG]) for i in range(2)]
        pinv = [sb(f"probinv{i}", [P, TG]) for i in range(2)]
        pT = [sb(f"pT{i}", [P, TG, 2, BLK]) for i in range(2)]
        sx = [sb(f"sx{i}", [P, ROWS]) for i in range(2)]
        y1 = [sb(f"y1_{i}", [P, ROWS]) for i in range(2)]
        y2 = [sb(f"y2_{i}", [P, ROWS]) for i in range(2)]
        up1 = [sb(f"up1_{i}", [P, ROWS]) for i in range(2)]
        b1_up, b2_up = sb("b1_up", [P, 1]), sb("b2_up", [P, 1])
        b1_s, b2_s, b2_all, b2_wide = sb("b1_s", [P, 1]), sb("b2_s", [P, 1]), sb("b2_all", [P, 1]), sb("b2_wide", [P, P])
        junk = sb("junk", [P, 2, TG, F])
        ssq = [sb(f"ssq{i}", [P, TG]) for i in range(2)]
        u = [sb(f"u{i}", [P, TG, F]) for i in range(4)]
        t1 = [sb(f"t{i}", [P, TG, F]) for i in range(2)]
        r = [sb(f"r{i}", [P, TG, F]) for i in range(2)]
        stats = sb("stats", [P, 2, TG, 6])
        mv = [sb(f"mv{i}", [P, TG, 2]) for i in range(2)]
        o = [sb(f"o{i}", [P, TG, F]) for i in range(4)]
        small = lambda n: [sb(f"{n}{i}", [P, 2, TG]) for i in range(2)]
        var, lnv, y0, y0sq, corr, rstd = (small(n) for n in ("var", "lnv", "y0_", "y0sq", "corr", "rstd"))
        nmr = [sb(f"nmr{i}", [P, TG]) for i in range(2)]

        pt_ps = ps("pt_ps", [P, 512])
        sx_ps, y1_ps, y2_ps = ps("sx_ps", [P, 512]), ps("y1_ps", [P, 512]), ps("y2_ps", [P, 512])
        z_ps = [ps(f"z_ps{i}", [P, TG, F]) for i in range(4)]

        wa_loaded = sem("wa_loaded")
        w_loaded = sem("w_loaded")
        b_loaded = sem("b_loaded")
        const_made = sem("const_made")
        W_turned = sem("W_turned")
        wa_done, ww1_done = sem("wa_done"), sem("ww1_done")
        b1w2_done, b2w3_done = sem("b1w2_done"), sem("b2w3_done")
        a_wide_made, WT_made, W2T_made = sem("a_wide_made"), sem("WT_made"), sem("W2T_made")
        wa_made = sem("wa_made")
        Wc_made, W3c_made, b1_made, ww1_made = sem("Wc_made"), sem("W3c_made"), sem("b1_made"), sem("ww1_made")
        b2_made, b3_made = sem("b2_made"), sem("b3_made")
        W23_made, b3c_made = sem("W23_made"), sem("b3c_made")
        W3_sum_made, W3_mean_made = sem("W3_sum_made"), sem("W3_mean_made")
        step = sem("step")
        x_loaded = [sem(f"x_loaded{i}") for i in range(4)]
        adj_loaded = [sem(f"adj_loaded{i}") for i in range(4)]
        stored = [sem(f"stored{i}") for i in range(4)]
        xw_made = sem("xw_made")
        e_summed = sem("e_summed")
        e_made = sem("e_made")
        scaled = sem("scaled")
        max_made = sem("max_made")
        shifted = sem("shifted")
        exp_made = sem("exp_made")
        sum_made = sem("sum_made")
        inv_made = sem("inv_made")
        prob_made = sem("prob_made")
        transposed = sem("transposed")
        pT_made = sem("pT_made")
        sx_done = sem("sx_done")
        sx_made = sem("sx_made")
        l1_done = sem("l1_done")
        up1_made = sem("up1_made")
        y1_made = sem("y1_made")
        l2_done = sem("l2_done")
        y2_made = sem("y2_made")
        z_done = sem("z_done")
        ssq_made = sem("ssq_made")
        u_made = sem("u_made")
        t_made = sem("t_made")
        r_made = sem("r_made")
        stats_made = sem("stats_made")
        mv_made = sem("mv_made")
        var_made = [sem(f"var_made{j}") for j in range(2)]
        ln_made, y0_made, sq_made, corr_made, rstd_made = (
            sem(n) for n in ("ln_made", "y0_made", "sq_made", "corr_made", "rstd_made"))
        nmr_made = sem("nmr_made")
        o_made = sem("o_made")
        o_last_made = sem("o_last_made")
        o_half_made = sem("o_half_made")

        x_flat = x.rearrange("b n f -> (b n) f")
        out_flat = out.rearrange("b n f -> (b n) f")

        def rows_of(flat, g):
            return bass.AP(tensor=flat.tensor, offset=g.i * (4 * ROWS * F) + g.k * (ROWS * F),
                           ap=[[F, P], [P * F, TG], [1, F]])

        def blocks_of(g, t):
            step = BLK * (N + 1)
            return bass.AP(tensor=adj.tensor, offset=g.batch() * (N * N) + ((g.k % GPB) * BG + t) * step,
                           ap=[[N, BLK], [2 * step, TG], [1, BLK]])

        def wide(v):
            return v[:, :].rearrange("p (s o) -> p s o", o=1).broadcast_to([P, TG, BLK])

        def each_tile(v):
            return v[:, :].rearrange("p (o f) -> p o f", o=1).broadcast_to([P, TG, F])

        block = ctx.enter_context(nc.Block())

        @block.sync
        def _(sync):
            def load(g):
                if not g.real():
                    return
                wait(sync, sx_done, g - 4)
                wait(sync, u_made, g - 4)
                sync.dma_start(xt[g.ring(4)][:, :, :], rows_of(x_flat, g)).then_inc(x_loaded[g.ring(4)], 16)
                wait(sync, scaled, g - 4)
                for t in range(2):
                    sync.dma_start(at[g.ring(4)][BLK * t:BLK * t + BLK, :, :],
                                   blocks_of(g, t)).then_inc(adj_loaded[g.ring(4)], 16)

            def slot(n):
                load(n + 4)
                g = n - 4
                if g.real():
                    if g.last():
                        sync.wait_ge(o_last_made, 2)
                    else:
                        wait(sync, o_made, g)
                        if g.last(1):
                            sync.wait_ge(o_half_made, 1)
                    sync.dma_start(rows_of(out_flat, g), o[g.ring(4)][:, :, :]).then_inc(stored[g.ring(4)], 16)

            for dst, src in ((W_sb, W), (a_sb, a)):
                sync.dma_start(dst[:, :], src[:, :]).then_inc(wa_loaded, 16)
            load(Group(0, 0))
            column = lambda v: v.rearrange("(p o) -> p o", o=1)
            everywhere = lambda v: v.rearrange("(o f) -> o f", o=1).broadcast_to([P, F])
            for dst, src in ((W1_sb, W1), (W2_sb, W2), (W3_sb, W3), (b1_sb, column(b1))):
                sync.dma_start(dst[:, :], src[:, :]).then_inc(w_loaded, 16)
            load(Group(0, 1))
            for dst, src in ((b2_sb, column(b2)), (b3_bc, everywhere(b3)), (b_bc, everywhere(ln_b)), (g_bc, everywhere(ln_g))):
                sync.dma_start(dst[:, :], src[:, :]).then_inc(b_loaded, 16)
            for k in range(2, FROM + 4):
                load(Group(0, k))
            slots(sync, slot, late=1)
            for k in range(4):
                sync.wait_ge(stored[k], 16 * (GROUPS // 4))

        @block.gpsimd
        def _(pool):
            pool.memset(ident[:, :], 0.0).then_inc(const_made, 1)
            pool.memset(ones_f[:, :], 1.0).then_inc(const_made, 1)
            pool.wait_ge(const_made, 1)
            pool.affine_select(out=ident[:, :], in_=ident[:, :], compare_op=ALU.not_equal, fill=1.0,
                               base=0, pattern=[[-1, P]], channel_multiplier=1).then_inc(const_made, 1)
            pool.memset(ones[:, :], 1.0).then_inc(const_made, 1)
            pool.memset(b3_rows[:, :], 0.0).then_inc(const_made, 1)
            for i in range(2):
                pool.memset(pT[i][:, :, :, :], 0.0).then_inc(const_made, 1)
            pool.wait_ge(wa_made, 1)

            def probabilities(g):
                if g.real():
                    wait(pool, inv_made, g)
                    pool.tensor_tensor(prob[g.ring(2)][:, :, :], prob[g.ring(2)][:, :, :],
                                       wide(pinv[g.ring(2)]), ALU.mult).then_inc(prob_made, 1)

            def scores(g):
                if g.real():
                    pool.wait_ge(adj_loaded[g.ring(4)], g.dma_done(2))
                    wait(pool, e_made, g)
                    pool.tensor_tensor(score[g.ring(2)][:, :, :], at[g.ring(4)][:, :, :],
                                       wide(e_lk[g.ring(2)]), ALU.mult).then_inc(scaled, 1)

            def x_times_wa(g):
                if g.real():
                    pool.wait_ge(x_loaded[g.ring(4)], g.dma_done())
                    pool.tensor_tensor(xw[g.ring(2)][:, :, :], xt[g.ring(4)][:, :, :], each_tile(wa_bc),
                                       ALU.mult).then_inc(xw_made, 1)

            def shifted_scores(g):
                if g.real():
                    wait(pool, max_made, g)
                    pool.tensor_tensor(score[g.ring(2)][:, :, :], score[g.ring(2)][:, :, :],
                                       wide(smax[g.ring(2)]), ALU.subtract).then_inc(shifted, 1)

            def o_ready(g):
                if g.real():
                    wait(pool, r_made, g)
                    if not isinstance(g.i, int) or g.k >= 4:
                        pool.wait_ge(stored[g.ring(4)], (g - 4).dma_done())

            def normalised(g):
                if g.real() and not g.last():
                    pool.wait_ge(const_made, 7)
                    wait(pool, nmr_made, g)
                    for s in range(TG // 2 if g.last(1) else TG):
                        last = pool.tensor_scalar(o[g.ring(4)][:, s, :], r[g.ring(2)][:, s, :],
                                                  rstd[(g + 1).ring(2)][:, 1, s:s + 1], nmr[g.ring(2)][:, s:s + 1],
                                                  op0=ALU.mult, op1=ALU.add)
                    last.then_inc(o_made, 1)

            def slot(n):
                o_ready(n - 4)
                x_times_wa(n + 3)
                scores(n + 2)
                probabilities(n + 1)
                normalised(n - 4)
                shifted_scores(n + 2)
            scores(Group(0, 0))
            shifted_scores(Group(0, 0))
            scores(Group(0, 1))
            probabilities(Group(0, 0))
            x_times_wa(Group(0, 2))
            shifted_scores(Group(0, 1))
            x_times_wa(Group(0, 3))
            probabilities(Group(0, 1))
            scores(Group(0, 2))
            shifted_scores(Group(0, 2))
            slots(pool, slot)

        @block.vector
        def _(dve):
            V = nc.vector
            steps = 0

            def then(instruction):
                nonlocal steps
                instruction.then_inc(step, 1)
                steps += 1
                dve.wait_ge(step, steps)

            def centre(j, src, dst, made):
                then(V.tensor_reduce(wmean[:, j:j + 1], src[:, :], op=ALU.add, axis=AX.X))
                then(V.tensor_scalar(wmean[:, j:j + 1], wmean[:, j:j + 1], 1.0 / F, None, op0=ALU.mult))
                V.tensor_scalar(dst[:, :], src[:, :], wmean[:, j:j + 1], None, op0=ALU.subtract).then_inc(made, 1)

            dve.wait_ge(wa_loaded, 32)
            dve.wait_ge(const_made, 7)
            V.tensor_scalar(a_wide[:, :], ones_f[:, :], a_sb[:, 0:1], None, op0=ALU.mult).then_inc(a_wide_made, 1)
            dve.wait_ge(W_turned, 1)
            V.tensor_copy(WT[:, :], sx_ps[:, 0:P]).then_inc(WT_made, 1)
            dve.wait_ge(wa_done, 1)
            V.tensor_copy(wa_bc[:, :], y1_ps[:, 0:F]).then_inc(wa_made, 1)

            def x_times_wa_first(g):
                dve.wait_ge(x_loaded[g.ring(4)], g.dma_done())
                wait(dve, wa_made, Group(0, 0))
                V.tensor_tensor(xw[g.ring(2)][:, :, :], xt[g.ring(4)][:, :, :], each_tile(wa_bc),
                                ALU.mult).then_inc(xw_made, 1)

            def b3_centred():
                dve.wait_ge(b_loaded, 16 * 4)
                centre(2, b3_bc, b3c, b3c_made)

            def second_layer():
                dve.wait_ge(b1w2_done, 1)
                V.tensor_scalar(W23[:, :], z_ps[1][:, 0, :], SLOPE, None, op0=ALU.mult).then_inc(W23_made, 1)
                then(V.tensor_tensor(b2_all[:, :], b2_sb[:, :], z_ps[1][:, 1, 0:1], ALU.add))
                then(V.tensor_scalar(b2_s[:, :], b2_all[:, :], SLOPE, None, op0=ALU.mult))
                V.tensor_scalar(b2_wide[:, :], ones_f[:, :], b2_s[:, 0:1], None, op0=ALU.mult).then_inc(b2_made, 1)
                V.tensor_scalar(b2_up[:, :], b2_all[:, :], 1 - SLOPE, None, op0=ALU.mult).then_inc(b2_made, 1)

            def third_layer():
                dve.wait_ge(b3c_made, 1)
                dve.wait_ge(b2w3_done, 1)
                then(V.tensor_tensor(b3_all[:, :], b3c[:, :], z_ps[0][:, 0, :], ALU.add))
                then(V.tensor_copy(b3_hi[:, :], b3_all[:, :]))
                V.tensor_copy(b3_rows[0:1, :], b3_hi[0:1, :]).then_inc(b3_made, 1)
                then(V.tensor_tensor(b3_rest[:, :], b3_all[:, :], b3_hi[:, :], ALU.subtract))
                then(V.tensor_copy(b3_mid[:, :], b3_rest[:, :]))
                V.tensor_copy(b3_rows[32:33, :], b3_mid[32:33, :]).then_inc(b3_made, 1)
                then(V.tensor_tensor(b3_rest2[:, :], b3_rest[:, :], b3_mid[:, :], ALU.subtract))
                V.tensor_copy(b3_rows[64:65, :], b3_rest2[64:65, :]).then_inc(b3_made, 1)

            def newton(g, step, norms=None, more=0):
                if not g.pair_real():
                    return
                q = g.ring(2)
                at = slice(*(norms or g.norms()))
                if step == 0:
                    wait(dve, y0_made, g + more)
                    V.tensor_tensor(y0sq[q][:, at, :], y0[q][:, at, :], y0[q][:, at, :], ALU.mult).then_inc(sq_made, 1)
                elif step == 1:
                    wait(dve, sq_made, g + more)
                    V.scalar_tensor_tensor(corr[q][:, at, :], y0sq[q][:, at, :], -0.5, var[q][:, at, :],
                                           op0=ALU.mult, op1=ALU.mult).then_inc(corr_made, 1)
                else:
                    wait(dve, corr_made, g + more)
                    V.scalar_tensor_tensor(rstd[q][:, at, :], corr[q][:, at, :], 1.5, y0[q][:, at, :],
                                           op0=ALU.add, op1=ALU.mult).then_inc(rstd_made, 1)

            def exp_sums(g):
                if g.real():
                    wait(dve, exp_made, g)
                    V.tensor_reduce(psum_[g.ring(2)][:, :], prob[g.ring(2)][:, :, :], op=ALU.add,
                                    axis=AX.X).then_inc(sum_made, 1)

            def inverses(g):
                if g.real():
                    wait(dve, sum_made, g)
                    V.reciprocal(pinv[g.ring(2)][:, :], psum_[g.ring(2)][:, :]).then_inc(inv_made, 1)

            def residual(g):
                if g.real():
                    V.tensor_tensor(u[g.ring(4)][:, :, :], xt[g.ring(4)][:, :, :], each_tile(b_bc),
                                    ALU.add).then_inc(u_made, 1)

            def maxima(g):
                if g.real():
                    wait(dve, scaled, g)
                    V.tensor_reduce(smax[g.ring(2)][:, :], score[g.ring(2)][:, :, :], op=ALU.max,
                                    axis=AX.X).then_inc(max_made, 1)

            def scaled_z(g):
                if g.real():
                    q = g.ring(2)
                    wait(dve, rstd_made, g)
                    for s in range(TG):
                        last = V.scalar_tensor_tensor(t1[q][:, s, :], z_ps[g.ring(4)][:, s, :],
                                                      rstd[q][:, 0, s:s + 1], g_bc[:, :], op0=ALU.mult, op1=ALU.mult)
                    last.then_inc(t_made, 1)

            def mean_times_rstd(g, more=0):
                if g.real():
                    wait(dve, rstd_made, g + 1 + more)
                    V.scalar_tensor_tensor(nmr[g.ring(2)][:, :], mv[g.ring(2)][:, :, 0], -1.0,
                                           rstd[(g + 1).ring(2)][:, 1, :], op0=ALU.mult, op1=ALU.mult).then_inc(nmr_made, 1)

            def r_sum(g):
                if g.real():
                    q = g.ring(2)
                    wait(dve, t_made, g)
                    wait(dve, o_made, g - 2)
                    V.tensor_tensor(r[q][:, :, :], t1[q][:, :, :], u[g.ring(4)][:, :, :], ALU.add).then_inc(r_made, 1)

            def first_variance(g):
                if g.real():
                    q = g.ring(2)
                    wait(dve, ssq_made, g)
                    V.tensor_scalar(var[q][:, 0, :], ssq[q][:, :], 1.0 / F, EPS, op0=ALU.mult,
                                    op1=ALU.add).then_inc(var_made[0], 1)

            def statistics(g):
                if g.real():
                    q = g.ring(2)
                    wait(dve, r_made, g)
                    for s in range(TG):
                        last = V.bn_stats(stats[:, q, s, :], r[q][:, s, :])
                    last.then_inc(stats_made, 1)

            def mean_variance(g):
                if g.real():
                    q = g.ring(2)
                    dve.wait_ge(const_made, 7)
                    wait(dve, stats_made, g)
                    for s in range(TG):
                        last = V.bn_aggr(mv[q][:, s, :], stats[:, q, s, :])
                    last.then_inc(mv_made, 1)

            def second_variance(g):
                if g.real():
                    wait(dve, mv_made, g)
                    V.tensor_scalar(var[(g + 1).ring(2)][:, 1, :], mv[g.ring(2)][:, :, 1], EPS, None,
                                    op0=ALU.add).then_inc(var_made[1], 1)

            def hidden_1(g):
                if g.real():
                    q = g.ring(2)
                    wait(dve, up1_made, g)
                    V.scalar_tensor_tensor(y1[q][:, :], y1_ps[:, :], SLOPE, up1[q][:, :],
                                           op0=ALU.mult, op1=ALU.add).then_inc(y1_made, 1)

            def leaky_e(g):
                if g.real():
                    q = g.ring(2)
                    wait(dve, e_summed, g)
                    V.scalar_tensor_tensor(e_lk[q][:, :], e_x[q][:, :], SLOPE_E, e_x[q][:, :],
                                           op0=ALU.mult, op1=ALU.max).then_inc(e_made, 1)

            def slot(n):
                exp_sums(n + 1)
                statistics(n - 3)
                mean_times_rstd(n - 4)
                leaky_e(n + 2)
                mean_variance(n - 3)
                first_variance(n - 2)
                inverses(n + 1)
                second_variance(n - 3)
                residual(n + 1)
                newton(n - 2, 0)
                newton(n - 2, 1)
                maxima(n + 2)
                newton(n - 2, 2)
                scaled_z(n - 2)
                hidden_1(n)
                r_sum(n - 2)

            x_times_wa_first(Group(0, 0))
            leaky_e(Group(0, 0))
            x_times_wa_first(Group(0, 1))
            maxima(Group(0, 0))
            centre(0, W_sb, Wc, Wc_made)
            leaky_e(Group(0, 1))
            exp_sums(Group(0, 0))
            inverses(Group(0, 0))
            maxima(Group(0, 1))
            b3_centred()
            second_layer()
            residual(Group(0, 0))
            exp_sums(Group(0, 1))
            inverses(Group(0, 1))
            leaky_e(Group(0, 2))
            third_layer()
            maxima(Group(0, 2))
            residual(Group(0, 1))
            hidden_1(Group(0, 0))
            slots(dve, slot, last=GROUPS)
            g = Group(0, GROUPS - 1)
            mean_times_rstd(g - 2)
            first_variance(g)
            statistics(g - 1)
            newton(g, 0, norms=(0, 1))
            mean_variance(g - 1)
            newton(g, 1, norms=(0, 1))
            second_variance(g - 1)
            newton(g, 2, norms=(0, 1))
            scaled_z(g)
            newton(g, 0, norms=(1, 2), more=1)
            r_sum(g)
            newton(g, 1, norms=(1, 2), more=1)
            statistics(g)
            newton(g, 2, norms=(1, 2), more=1)
            mean_variance(g)
            mean_times_rstd(g - 1, more=1)
            second_variance(g)
            for k in range(3):
                newton(g + 1, k, more=1)
            mean_times_rstd(g, more=1)
            wait(dve, nmr_made, g)
            dve.wait_ge(stored[g.ring(4)], (g - 4).dma_done())
            for s in range(TG // 2):
                last = V.tensor_scalar(o[g.ring(4)][:, s, :], r[g.ring(2)][:, s, :], rstd[(g + 1).ring(2)][:, 1, s:s + 1],
                                       nmr[g.ring(2)][:, s:s + 1], op0=ALU.mult, op1=ALU.add)
            last.then_inc(o_last_made, 1)

        @block.scalar
        def _(act):
            S = nc.scalar
            act.preload_act_table_set("natural_log_exp_and_others")

            def root(g, norms=None):
                if g.pair_real():
                    q = g.ring(2)
                    at = slice(*(norms or g.norms()))
                    if at.stop == 2:
                        wait(act, var_made[1], g - 1)
                    else:
                        wait(act, var_made[0], g)
                    S.activation(lnv[q][:, at, :], var[q][:, at, :], ACT.Ln).then_inc(ln_made, 1)

            def root_exp(g, norms=None, more=0):
                if g.pair_real():
                    q = g.ring(2)
                    at = slice(*(norms or g.norms()))
                    wait(act, ln_made, g + more)
                    S.activation(y0[q][:, at, :], lnv[q][:, at, :], ACT.Exp, scale=-0.5).then_inc(y0_made, 1)

            def squares(g, tiles):
                if g.real():
                    q = g.ring(2)
                    wait(act, z_done, g)
                    for s in tiles:
                        last = S.activation(junk[:, q, s, :], z_ps[g.ring(4)][:, s, :], ACT.Square,
                                            accum_out=ssq[q][:, s:s + 1])
                    if TG - 1 in tiles:
                        last.then_inc(ssq_made, 1)

            def sx_copy(g):
                if g.real():
                    wait(act, sx_done, g)
                    S.activation(sx[g.ring(2)][:, :], sx_ps[:, :], ACT.Copy).then_inc(sx_made, 1)

            def up_2(g):
                if g.real():
                    wait(act, l2_done, g)
                    S.activation(y2[g.ring(2)][:, :], y2_ps[:, :], ACT.Relu, bias=b2_up[:, 0:1],
                                 scale=1 - SLOPE).then_inc(y2_made, 1)

            def up_1(g):
                if g.real():
                    wait(act, l1_done, g)
                    S.activation(up1[g.ring(2)][:, :], y1_ps[:, :], ACT.Relu, bias=b1_up[:, 0:1],
                                 scale=1 - SLOPE).then_inc(up1_made, 1)

            def prob_copy(g):
                if g.real():
                    wait(act, transposed, g)
                    for half in range(2):
                        for t in range(2):
                            last = S.activation(
                                pT[g.ring(2)][BLK * t:BLK * t + BLK, half:TG:2, t, :],
                                pt_ps[BLK * half:BLK * half + BLK, 0:2 * P].rearrange(
                                    "p (h t i) -> p h t i", h=2, t=2)[:, :, t, :], ACT.Copy)
                    last.then_inc(pT_made, 1)

            def e_sums(g, tiles):
                if g.real():
                    q = g.ring(2)
                    wait(act, xw_made, g)
                    for s in tiles:
                        last = S.activation(xw[q][:, s, :], xw[q][:, s, :], ACT.Identity, accum_out=e_x[q][:, s:s + 1])
                    if TG - 1 in tiles:
                        last.then_inc(e_summed, 1)

            def exponentials(g):
                if g.real():
                    wait(act, shifted, g)
                    S.activation(prob[g.ring(2)][:, :, :], score[g.ring(2)][:, :, :], ACT.Exp).then_inc(exp_made, 1)

            def first_layer():
                act.wait_ge(w_loaded, 16 * 4)
                act.wait_ge(ww1_done, 1)
                S.activation(WW1[:, :], y2_ps[:, 0:F], ACT.Copy).then_inc(ww1_made, 1)
                S.activation(W3_copy[:, :], W3_sb[:, :], ACT.Identity, accum_out=wmean[:, 1:2]).then_inc(W3_sum_made, 1)
                S.activation(W2T[:, :], z_ps[0][:, 0, :], ACT.Copy).then_inc(W2T_made, 1)
                act.wait_ge(W3_sum_made, 1)
                S.activation(wmean[:, 3:4], wmean[:, 1:2], ACT.Copy, scale=-1.0 / F).then_inc(W3_mean_made, 1)
                S.activation(b1_s[:, :], b1_sb[:, :], ACT.Copy, scale=SLOPE).then_inc(b1_made, 1)
                S.activation(b1_up[:, :], b1_sb[:, :], ACT.Copy, scale=1 - SLOPE).then_inc(b1_made, 1)
                act.wait_ge(W3_mean_made, 1)
                S.activation(W3c[:, :], W3_copy[:, :], ACT.Identity, bias=wmean[:, 3:4]).then_inc(W3c_made, 1)

            def slot(n):
                exponentials(n + 1)
                e_sums(n + 2, (2, 3))
                squares(n - 2, (0, 1))
                squares(n - 2, (2, 3))
                sx_copy(n)
                root(n - 2)
                root_exp(n - 2)
                up_2(n - 1)
                e_sums(n + 3, (0, 1))
                up_1(n)
                prob_copy(n + 1)

            e_sums(Group(0, 0), (0, 1))
            e_sums(Group(0, 0), (2, 3))
            first_layer()
            e_sums(Group(0, 1), (0, 1))
            e_sums(Group(0, 1), (2, 3))
            exponentials(Group(0, 0))
            prob_copy(Group(0, 0))
            e_sums(Group(0, 2), (0, 1))
            exponentials(Group(0, 1))
            e_sums(Group(0, 2), (2, 3))
            sx_copy(Group(0, 0))
            e_sums(Group(0, 3), (0, 1))
            prob_copy(Group(0, 1))
            act.wait_ge(b1_made, 2)
            up_1(Group(0, 0))
            act.wait_ge(b2_made, 2)
            slots(act, slot, last=GROUPS)
            g = Group(0, GROUPS - 1)
            squares(g, range(TG))
            root(g, norms=(0, 1))
            root_exp(g, norms=(0, 1))
            root(g, norms=(1, 2))
            root_exp(g, norms=(1, 2), more=1)
            root(g + 1)
            root_exp(g + 1, more=1)

            def normalised_half(g, made):
                act.wait_ge(stored[g.ring(4)], (g - 4).dma_done())
                wait(act, nmr_made, g)
                for s in range(TG // 2, TG):
                    last = S.activation(o[g.ring(4)][:, s, :], r[g.ring(2)][:, s, :], ACT.Identity,
                                        scale=rstd[(g + 1).ring(2)][:, 1, s:s + 1], bias=nmr[g.ring(2)][:, s:s + 1])
                last.then_inc(made, 1)

            normalised_half(g - 1, o_half_made)
            normalised_half(g, o_last_made)

        @block.tensor
        def _(pe):
            T = nc.tensor
            pe.wait_ge(wa_loaded, 32)
            pe.wait_ge(const_made, 3)
            T.transpose(sx_ps[:, 0:P], W_sb[:, :], ident[:, :]).then_inc(W_turned, 1)
            pe.wait_ge(a_wide_made, 1)
            pe.wait_ge(WT_made, 1)
            T.matmul(y1_ps[:, 0:F], a_wide[:, :], WT[:, :], start=True, stop=True).then_inc(wa_done, 1)
            pe.wait_ge(w_loaded, 16 * 4)
            T.transpose(z_ps[0][:, 0, :], W2_sb[:, :], ident[:, :])
            T.matmul(y2_ps[:, 0:F], WT[:, :], W1_sb[:, :], start=True, stop=True).then_inc(ww1_done, 1)

            def w2_products():
                pe.wait_ge(W2T_made, 1)
                pe.wait_ge(W3c_made, 1)
                T.matmul(z_ps[1][:, 0, :], W2T[:, :], W3c[:, :], start=True, stop=True)
                T.matmul(z_ps[1][:, 1, 0:1], W2_sb[:, :], b1_s[:, :], start=True, stop=True).then_inc(b1w2_done, 1)

            def keep_busy(products):
                for _ in range(products):
                    T.matmul(z_ps[3][:, :, :], ones[:, :], each_tile(ones), start=True, stop=True)

            def b2_on_w3():
                pe.wait_ge(b2_made, 1)
                T.matmul(z_ps[0][:, 0, :], b2_wide[:, :], W3c[:, :], start=True, stop=True).then_inc(b2w3_done, 1)

            def layer(out_ps, weights, rhs):
                return T.matmul(out_ps[:, :], weights[:, :], rhs[:, :], start=True, stop=True)

            def attend(g):
                if g.real():
                    wait(pe, pT_made, g)
                    for s in range(TG):
                        last = T.matmul(sx_ps[:, s * P:(s + 1) * P], xt[g.ring(4)][:, s, :],
                                        pT[g.ring(2)][:, s, :, :].rearrange("p t i -> p (t i)"), start=True, stop=True)
                    last.then_inc(sx_done, 1)

            def layer_2(g):
                if g.real():
                    wait(pe, y1_made, g)
                    layer(y2_ps, W2_sb, y1[g.ring(2)]).then_inc(l2_done, 1)

            def layer_1(g):
                if g.real():
                    wait(pe, sx_made, g)
                    layer(y1_ps, WW1, sx[g.ring(2)]).then_inc(l1_done, 1)

            def turn(g):
                if g.real():
                    wait(pe, prob_made, g)
                    for h in range(2):
                        last = T.transpose(pt_ps[:, h * P:(h + 1) * P],
                                           prob[g.ring(2)][:, 2 * h:2 * h + 2, :].rearrange("p t j -> p (t j)"),
                                           ident[:, :])
                    last.then_inc(transposed, 1)

            def rows_times(g, lhs, weights, tiles=range(TG), stop=False):
                for s in tiles:
                    last = T.matmul(z_ps[g.ring(4)][:, s, :], lhs[g.ring(2)][:, s * P:(s + 1) * P], weights[:, :],
                                    start=False, stop=stop and s == TG - 1)
                return last

            def z_of_sx(g):
                if g.real():
                    T.matmul(z_ps[g.ring(4)][:, :, :], ones[:, :],
                             each_tile(b3_rows), start=True, stop=False)
                    rows_times(g, sx, Wc)

            def z_of_y1(g, tiles):
                if g.real():
                    rows_times(g, y1, W23, tiles)

            def z_of_y2(g):
                if g.real():
                    wait(pe, y2_made, g)
                    rows_times(g, y2, W3c, stop=True).then_inc(z_done, 1)

            def slot(n):
                z_of_sx(n - 1)
                attend(n)
                layer_2(n - 1)
                z_of_y1(n - 1, (0, 1))
                layer_1(n)
                z_of_y1(n - 1, (2, 3))
                turn(n + 1)
                z_of_y2(n - 1)

            keep_busy(4)
            w2_products()
            keep_busy(6)
            turn(Group(0, 0))
            attend(Group(0, 0))
            b2_on_w3()
            pe.wait_ge(ww1_made, 1)
            layer_1(Group(0, 0))
            turn(Group(0, 1))
            pe.wait_ge(Wc_made, 1)
            pe.wait_ge(W23_made, 1)
            pe.wait_ge(b3_made, 3)
            slots(pe, slot)


_NAMES = ["x", "adj"] + ["L0_gnn_" + n for n in ("W", "a", "ln_g", "ln_b", "W1", "b1", "W2", "b2", "W3", "b3")]


def kernel(**inputs):
    import numpy as np
    import concourse.bacc as bacc
    from concourse.bass_utils import run_bass_kernel_spmd

    nc = bacc.Bacc("TRN2", target_bir_lowering=False, num_devices=1)
    arrays, args = {}, []
    for name in _NAMES:
        array = np.ascontiguousarray(inputs[name])
        arrays[f"in_{name}"] = array
        args.append(nc.dram_tensor(f"in_{name}", array.shape, mybir.dt.from_np(array.dtype), kind="ExternalInput").ap())
    args.append(nc.dram_tensor("out", (B, N, F), mybir.dt.float32, kind="ExternalOutput").ap())
    program(nc, *args)
    done = run_bass_kernel_spmd(nc, [arrays], core_ids=[0])
    return done.results[0]["out"]
```
